# Optimizing a Trainium2 kernel written in Bass

```python
import numpy as np
import jax
import jax.numpy as jnp

def _softmax(x, axis=-1):
    return jax.nn.softmax(x, axis=axis)

def _gelu(x):
    return jax.nn.gelu(x, approximate=True)

def _silu(x):
    return jax.nn.silu(x)

def _sigmoid(x):
    return jax.nn.sigmoid(x)

def _layernorm(x, axis=-1, eps=1e-05):
    m = jnp.mean(x, axis=axis, keepdims=True)
    v = jnp.var(x, axis=axis, keepdims=True)
    return (x - m) / jnp.sqrt(v + eps)

def _scatter_add(tgt, idx, src, axis=0):
    return tgt.at[idx].add(src)

def _segment_sum(src, seg, n):
    return jax.ops.segment_sum(src, seg, n)
kernel_name = 'mk_seq_preln_d1_jaxref_r8_c0f5d7'

def setup_inputs(seed: int=0):
    np.random.seed(seed)
    _w = jnp.asarray

    def _L0_attn_setup():
        import jax, jax.numpy as jnp
        import numpy as np
        EPS = 1e-08

        def log_g(x):
            return jnp.where(x >= 0, jnp.log(jax.nn.relu(x) + 0.5 + EPS), -jax.nn.softplus(-x) + EPS)
        key = jax.random.key(seed)
        k_x, k_w = jax.random.split(key)
        B, S, D, H = (8, 512, 128, 128)
        x_t = jax.random.normal(k_x, (B, S, D), dtype=jnp.float32)
        std = np.sqrt(2.0 / (5.0 * (3 * H)))
        W = jax.random.normal(k_w, (3 * H, D), dtype=jnp.float32) * std
        return {'x_t': x_t, 'W': W}
    _L0_attn_in = _L0_attn_setup()

    def _L0_ffn_setup():
        import jax, jax.numpy as jnp
        import numpy as np
        B, S, D, E, F = (2, 256, 128, 8, 512)
        key = jax.random.key(seed)
        k1, k2, k3, k4 = jax.random.split(key, 4)
        x = jax.random.normal(k1, (B, S, D), dtype=jnp.float32)
        gate_w = jax.random.normal(k2, (E, D), dtype=jnp.float32) * 0.02
        w1 = jax.random.normal(k3, (E, D, F), dtype=jnp.float32) * 0.02
        w2 = jax.random.normal(k4, (E, F, D), dtype=jnp.float32) * 0.02
        return {'x': x, 'gate_w': gate_w, 'w1': w1, 'w2': w2}
    _L0_ffn_in = _L0_ffn_setup()
    _d = {'L0_attn_x_t': _L0_attn_in['x_t'], 'L0_attn_W': _L0_attn_in['W'], 'L0_ffn_gate_w': _L0_ffn_in['gate_w'], 'L0_ffn_w1': _L0_ffn_in['w1'], 'L0_ffn_w2': _L0_ffn_in['w2']}
    _x0 = _d['L0_attn_x_t']
    _d['L0_attn_x_t'] = jax.random.normal(jax.random.fold_in(jax.random.key(seed), 1), (16, 256, 128), dtype=_x0.dtype)
    del _x0
    return _d

def reference(L0_attn_x_t, L0_attn_W, L0_ffn_gate_w, L0_ffn_w1, L0_ffn_w2):

    def _L0_attn_ref(x_t, W):
        import jax, jax.numpy as jnp
        import numpy as np
        EPS = 1e-08

        def log_g(x):
            return jnp.where(x >= 0, jnp.log(jax.nn.relu(x) + 0.5 + EPS), -jax.nn.softplus(-x) + EPS)
        H = W.shape[0] // 3
        gates = jnp.einsum('bsd,hd->bsh', x_t, W)
        f_gate = gates[..., :H]
        i_gate = gates[..., H:2 * H]
        hidden = gates[..., 2 * H:]
        diff = jax.nn.softplus(-f_gate) - jax.nn.softplus(-i_gate)
        log_f = -jax.nn.softplus(diff)
        log_i = -jax.nn.softplus(-diff)
        log_tilde_h = log_g(hidden)
        log_values = log_i + log_tilde_h
        log_coeffs = log_f
        a_star = jnp.cumsum(log_coeffs + EPS, axis=1)
        log_h0_plus_b_star = jax.lax.cumlogsumexp(log_values - a_star, axis=1)
        h_t = jnp.exp(a_star + log_h0_plus_b_star)
        return h_t

    def _L0_ffn_ref(x, gate_w, w1, w2):
        import jax, jax.numpy as jnp
        import numpy as np
        B, S, D, E, F = (2, 256, 128, 8, 512)
        b, s, d = x.shape
        n_experts = w1.shape[0]
        tokens = x.reshape(-1, d)
        logits = tokens @ gate_w.T
        expert_ids = jnp.argmax(logits, axis=-1)
        dispatch = jax.nn.one_hot(expert_ids, n_experts, dtype=tokens.dtype)
        h = jnp.einsum('td,edf->etf', tokens, w1)
        h = jax.nn.gelu(h, approximate=False)
        out_e = jnp.einsum('etf,efd->etd', h, w2)
        out = jnp.einsum('etd,te->td', out_e, dispatch)
        return out.reshape(b, s, d)
    x = L0_attn_x_t
    x = x + _L0_attn_ref(_layernorm(x, axis=-1), L0_attn_W)
    x = x + _L0_ffn_ref(_layernorm(x, axis=-1), L0_ffn_gate_w, L0_ffn_w1, L0_ffn_w2)
    return x

_drawn_inputs = setup_inputs


def setup_inputs(seed=0):
    import zlib

    import numpy as np

    out = dict(_drawn_inputs(seed))
    spreads = {}
    factors = {}
    for name, (base, spread) in spreads.items():
        noise = np.random.default_rng([zlib.crc32(name.encode()), seed]).standard_normal(out[name].shape)
        drawn = base * np.exp(spread * noise) if base else spread * noise
        out[name] = jnp.asarray(drawn.astype(out[name].dtype))
    for name, factor in factors.items():
        out[name] = (out[name] * factor).astype(out[name].dtype)
    return out
```

```python
import concourse.bass as bass
from concourse import mybir
from contextlib import ExitStack


def build_gru_and_routed_ffn(nc, x_in, W_in, gate_w_in, w1_in, w2_in, out):
    f32, bf16, i32, u32 = mybir.dt.float32, mybir.dt.bfloat16, mybir.dt.int32, mybir.dt.uint32
    ALU, ACT, AX = mybir.AluOpType, mybir.ActivationFunctionType, mybir.AxisListType
    P = 128
    B, S, D = x_in.shape
    H = W_in.shape[0] // 3
    E, _, F = w1_in.shape
    T = B * S
    NT = T // P
    BT = 4
    N = BT * P
    NB = NT // BT
    FC = F // P
    NS = NT + E - 1
    RING = 6
    NO_TOKEN = 2 * T
    LN_EPS, EPS = 1e-5, 1e-8
    BIG = 1e30

    x_rows = x_in.rearrange("b s d -> (b s) d")
    x_tiles = x_rows.rearrange("(n p) d -> p n d", p=P)
    out_rows = out.rearrange("b s d -> (b s) d")
    rows = nc.dram_tensor("x2_and_normed", (T, 2 * D), f32, kind="Internal").ap()
    rows_tiles = rows.rearrange("(n p) c -> p n c", p=P)

    ctx = ExitStack()
    with ctx:
        def sb(name, shape, dt=f32):
            return ctx.enter_context(nc.sbuf_tensor(name, shape, dt))

        def sem(name):
            return ctx.enter_context(nc.semaphore(name))

        ident = sb("ident", [P, P])
        ones = sb("ones", [P, P], bf16)
        before = sb("before", [P, P], bf16)
        scan_ones = sb("scan_ones", [P, NT])
        neg_half = sb("neg_half", [P, BT])
        ln_eps = sb("ln_eps", [P, BT])
        halves = sb("halves", [P, BT, 2])
        prefer_first = sb("prefer_first", [P, E])
        row_no = sb("row_no", [P, P], bf16)
        slot_no = sb("slot_no", [P, NS])
        tile_shifted = sb("tile_shifted", [P, NT])
        part_no = sb("part_no", [P, 1])
        W_nat = sb("W_nat", [P, 3, D])
        WT = sb("WT", [P, 3, H])
        gw_nat = sb("gw_nat", [E, D])
        gwT = sb("gwT", [P, E])
        w1 = sb("w1", [P, E * F])
        w2 = sb("w2", [P, E * FC * D])
        x = sb("x", [P, NT, D])
        st1, st2 = sb("st1", [P, 2, BT, 6]), sb("st2", [P, 2, BT, 6])
        sq1, sq2 = sb("sq1", [P, BT, 2]), sb("sq2", [P, BT, 2])
        mv1, mv2 = sb("mv1", [P, 2, BT, 2]), sb("mv2", [P, 2, BT, 2])
        dm1, dm2 = sb("dm1", [P, BT]), sb("dm2", [P, BT])
        dd1, dd2 = sb("dd1", [P, BT]), sb("dd2", [P, BT])
        va1, va2 = sb("va1", [P, BT]), sb("va2", [P, BT])
        ve1, ve2 = sb("ve1", [P, BT]), sb("ve2", [P, BT])
        rstd1, rstd2 = sb("rstd1", [P, 2, BT]), sb("rstd2", [P, 2, BT])
        xn = sb("xn", [P, 2, BT, D])
        xnT = sb("xnT", [P, 2, N])
        xn2T = sb("xn2T", [P, 2, N])
        L = sb("L", [P, 2, 3, N])
        pos = sb("pos", [P, 2, N])
        ls = sb("ls", [P, 2, 3, N])
        RS = sb("RS", [P, 2, 2, N])
        den = sb("den", [P, 2, N])
        Fg = sb("Fg", [P, 2, N])
        Ig = sb("Ig", [P, 2, N])
        val = sb("val", [P, 2, N])
        h = sb("h", [P, 2, N])
        x2n = sb("x2n", [P, 2, BT, 2 * D])
        lg = sb("lg", [P, NT, E])
        best = sb("best", [P, NT])
        tied = sb("tied", [P, NT, E])
        pref = sb("pref", [P, NT, E])
        bestp = sb("bestp", [P, NT])
        O = sb("O", [P, NT, E], bf16)
        tot = sb("tot", [P, NT, E])
        cum = sb("cum", [P, NT, E])
        excl = sb("excl", [P, NT, E])
        rank3 = sb("rank3", [P, NT, E])
        sel = sb("sel", [P, NT, E])
        rank_i = sb("rank_i", [P, NT], i32)
        rdiv_i = sb("rdiv_i", [P, NT], i32)
        rmod_i = sb("rmod_i", [P, NT], i32)
        rmod = sb("rmod", [P, NT])
        nt_i = sb("nt_i", [P, E], i32)
        nt_sh = sb("nt_sh", [P, E], i32)
        nt_f = sb("nt_f", [P, E])
        cs = sb("cs", [P, E])
        base = sb("base", [P, E])
        sbase = sb("sbase", [P, NT, E])
        slot0 = sb("slot0", [P, NT])
        slot = sb("slot", [P, NT])
        past = sb("past", [1, NS, E])
        eid_f = sb("eid_f", [1, NS])
        eid = sb("eid", [1, NS], i32)
        OJ = sb("OJ", [P, NT, P], bf16)
        S1 = sb("S1", [P, NT, NS], bf16)
        SM = sb("SM", [P, NT, 2, NS], bf16)
        low = sb("low", [P, NS])
        ids = sb("ids", [P, NS], i32)
        xg = [sb(f"xg{k}", [P, 2 * D]) for k in range(RING)]
        xgT = sb("xgT", [P, 2, P])
        hid = sb("hid", [P, 2, F])
        hidT = sb("hidT", [P, 2, F])
        yo = [sb(f"yo{k}", [P, D]) for k in range(RING)]

        psum = [ctx.enter_context(nc.psum_tensor(f"bank{k}", [P, 512], f32)) for k in range(2)]
        gates = [ctx.enter_context(nc.psum_tensor(f"gates{k}", [P, 3, N], f32)) for k in range(2)]
        T1, T2 = psum[0], psum[1]
        PU, PHT, PY = (gates[0][:, k, :] for k in range(3))
        PXT, PR, PI = (gates[1][:, k, :] for k in range(3))

        names = """const_row const_dve ident_zero tri_zero W_loaded gw_loaded w1_loaded w2_loaded WT_ready WT_sb
        stats1 ln1 rstd1_done norm1 xT_ready xT_sb gates_done absd expd lnd ls_done dl_done exp2_done
        g_done den_done F_done I_done v_done scan_done hb_ready x2_done stats2 ln2 rstd2_done norm2
        x2T_ready x2T_sb lg_ready lg_sb route counts_ready S1_done OJ_done SM_done ids_ready ids_done slots_done
        xgT_ready xgT_sb up_done gelu_done hT_ready hT_sb y_ready y_done xg_zero""".split()
        s = {n: sem(n) for n in names}
        x_loaded = [sem(f"x_loaded{k}") for k in range(2)]
        rows_stored = [sem(f"rows_stored{k}") for k in range(2)]
        gathered = [sem(f"gathered{k}") for k in range(RING)]
        scattered = [sem(f"scattered{k}") for k in range(RING)]

        def wait(eng, name, value):
            if type(value) is not int or value > 0:
                eng.wait_ge(s[name] if type(name) is str else name, value)

        def blocks(eng, body):
            for i in range(-2, 2):
                body(i // 2, i % 2)
            with eng.Fori(1, NB // 2 - 1) as j:
                body(j, 0)
                body(j, 1)
            for i in range(NB - 2, NB + 1):
                body(i // 2, i % 2)

        def at(j, q, ahead):
            k = q + ahead
            jj, qq = j + k // 2, k % 2
            b = 2 * jj + qq
            if type(b) is int and not 0 <= b < NB:
                return None
            return b, qq, jj

        LOOPED = NS // RING * RING

        def slots(eng, body):
            body(0, 0, RING)
            with eng.Fori(1, NS // RING - 1) as j:
                body(j, 0, RING)
            body(NS // RING - 1, 0, RING)
            body(NS // RING, 0, NS - LOOPED)

        def exists(n):
            return type(n) is not int or 0 <= n < NS

        block = ctx.enter_context(nc.Block())

        @block.sync
        def _(sp):
            sp.dma_start(W_nat[:], W_in.rearrange("(g p) d -> p g d", p=P)).then_inc(s["W_loaded"], 16)
            sp.dma_start(gw_nat[:], gate_w_in).then_inc(s["gw_loaded"], 16)
            for b in range(NB):
                wait(sp, x_loaded[b % 2], 16 * (b // 2))
                sp.dma_start(x[:, b * BT:(b + 1) * BT, :], x_tiles[:, b * BT:(b + 1) * BT, :]).then_inc(x_loaded[b % 2], 16)
            sp.dma_start(w1[:].rearrange("p (e f) -> p e f", e=E), w1_in.rearrange("e d f -> d e f")).then_inc(s["w1_loaded"], 16)
            sp.dma_start(w2[:].rearrange("p (e c d) -> p e c d", e=E, c=FC),
                         w2_in.rearrange("e (c p) d -> p e c d", p=P)).then_inc(s["w2_loaded"], 16)

            with sp.Fori(0, NB // 2) as j:
                for q in range(2):
                    b = 2 * j + q
                    sp.wait_ge(s["norm2"], b + 1)
                    sp.dma_start(rows_tiles[:, bass.ds(b * BT, BT), :], x2n[:, q]).then_inc(rows_stored[q], 16)

        @block.gpsimd
        def _(pool):
            pool.memset(ident[:], 0.0).then_inc(s["ident_zero"], 1)
            pool.memset(before[:], 1.0).then_inc(s["tri_zero"], 1)
            pool.wait_ge(s["ident_zero"], 1)
            pool.affine_select(out=ident[:], in_=ident[:], compare_op=ALU.not_equal, fill=1.0, base=0,
                               pattern=[[-1, P]], channel_multiplier=1).then_inc(s["const_row"], 1)
            pool.memset(neg_half[:], -0.5).then_inc(s["const_row"], 1)
            pool.memset(ln_eps[:], LN_EPS).then_inc(s["const_row"], 1)
            pool.memset(halves[:, :, 0], 0.5).then_inc(s["const_row"], 1)
            pool.memset(halves[:, :, 1], 1.0 / D).then_inc(s["const_row"], 1)

            def rstd(b, q, stats, st, sq, mv, dm, dd, va, ve, r, ln, done):
                steps = 6
                wait(pool, stats, b + 1)
                pool.tensor_tensor(sq[:], st[:, q, :, 1:3], st[:, q, :, 4:6], ALU.add).then_inc(s[ln], 1)
                wait(pool, ln, steps * b + 1)
                pool.tensor_tensor(mv[:, q], sq[:], halves[:], ALU.mult).then_inc(s[ln], 1)
                wait(pool, ln, steps * b + 2)
                pool.tensor_tensor(dm[:], st[:, q, :, 1], mv[:, q, :, 0], ALU.subtract).then_inc(s[ln], 1)
                wait(pool, ln, steps * b + 3)
                pool.tensor_tensor(dd[:], dm[:], dm[:], ALU.mult).then_inc(s[ln], 1)
                wait(pool, ln, steps * b + 4)
                pool.tensor_tensor(va[:], mv[:, q, :, 1], dd[:], ALU.add).then_inc(s[ln], 1)
                wait(pool, ln, steps * b + 5)
                pool.tensor_tensor(ve[:], va[:], ln_eps[:], ALU.add).then_inc(s[ln], 1)
                wait(pool, ln, steps * b + 6)
                pool.tensor_tensor(r[:, q], ve[:], neg_half[:], ALU.pow).then_inc(s[done], 1)

            pool.wait_ge(s["const_row"], 5)

            def step(j, q):
                if k := at(j, q, 0):
                    b, p, _ = k
                    wait(pool, "ls_done", b + 1)
                    pool.tensor_tensor(ls[:, p, 1], ls[:, p, 1], ls[:, p, 0], ALU.subtract).then_inc(s["dl_done"], 1)
                if k := at(j, q, -1):
                    rstd(k[0], k[1], "stats2", st2, sq2, mv2, dm2, dd2, va2, ve2, rstd2, "ln2", "rstd2_done")
                if k := at(j, q, 2):
                    rstd(k[0], k[1], "stats1", st1, sq1, mv1, dm1, dd1, va1, ve1, rstd1, "ln1", "rstd1_done")
                if k := at(j, q, 0):
                    b, p, _ = k
                    wait(pool, "exp2_done", b + 1)
                    pool.tensor_tensor(pos[:, p], pos[:, p], RS[:, p, 1], ALU.add).then_inc(s["g_done"], 1)
                    wait(pool, "g_done", b + 1)
                    wait(pool, "I_done", b + 1)
                    wait(pool, "scan_done", b - 1)
                    pool.tensor_tensor(val[:, p], pos[:, p], Ig[:, p], ALU.mult).then_inc(s["v_done"], 1)

            blocks(pool, step)
            pool.wait_ge(s["tri_zero"], 1)
            pool.affine_select(out=before[:], in_=before[:], compare_op=ALU.is_gt, fill=0.0, base=0,
                               pattern=[[1, P]], channel_multiplier=-1).then_inc(s["const_row"], 1)
            pool.iota(row_no[:], [[1, P]], base=0, channel_multiplier=0, allow_small_or_imprecise_dtypes=True).then_inc(s["const_row"], 1)
            pool.iota(slot_no[:], [[1, NS]], base=0, channel_multiplier=0, allow_small_or_imprecise_dtypes=True).then_inc(s["const_row"], 1)
            pool.iota(tile_shifted[:], [[1, NT]], base=-(NO_TOKEN // P), channel_multiplier=0, allow_small_or_imprecise_dtypes=True).then_inc(s["const_row"], 1)
            pool.iota(part_no[:], [[0, 1]], base=0, channel_multiplier=1, allow_small_or_imprecise_dtypes=True).then_inc(s["const_row"], 1)
            pool.iota(prefer_first[:], [[-1, E]], base=E, channel_multiplier=0, allow_small_or_imprecise_dtypes=True).then_inc(s["const_row"], 1)
            for k in range(RING):
                pool.memset(xg[k][:], 0.0).then_inc(s["xg_zero"], 1)

            last_token = pool.to_reg(T - 1)

            def gather(n):
                k = n % RING
                pool.indirect_dma_start(xg[k][:], None, rows, bass.IndirectOffsetOnAxis(ids[:, n:n + 1], 0),
                                        bounds_check=last_token, oob_is_err=False).then_inc(gathered[k], 16)

            def scatter(n):
                k = n % RING
                pool.wait_ge(s["y_done"], n + 1)
                pool.indirect_dma_start(out_rows, bass.IndirectOffsetOnAxis(ids[:, n:n + 1], 0), yo[k][:], None,
                                        bounds_check=last_token, oob_is_err=False).then_inc(scattered[k], 16)

            pool.wait_ge(s["xg_zero"], RING)
            for q in range(2):
                pool.wait_ge(rows_stored[q], 16 * (NB // 2))
            pool.wait_ge(s["ids_done"], 1)
            for n in range(RING):
                gather(n)
            for n in range(NS):
                scatter(n)
                if n + RING < NS:
                    gather(n + RING)
            for k in range(RING):
                pool.wait_ge(scattered[k], 16 * ((NS - 1 - k) // RING + 1))

        @block.scalar
        def _(act):
            def copy_WT():
                act.wait_ge(s["WT_ready"], 1)
                act.activation(WT[:].rearrange("p g h -> p (g h)"), T1[:, 0:3 * H], ACT.Copy)
                act.activation(gwT[:], T1[:, 3 * H:3 * H + E], ACT.Copy).then_inc(s["WT_sb"], 1)

            def step(j, q):
                if k := at(j, q, 1):
                    b, p, _ = k
                    wait(act, "gates_done", b + 1)
                    wait(act, "v_done", b - 1)
                    act.activation(pos[:, p], gates[p][:, 2, :], ACT.Relu)
                    act.activation(L[:, p, 2], gates[p][:, 2, :], ACT.Relu, scale=-1.0)
                    act.activation(L[:, p, 0:2], gates[p][:, 0:2, :], ACT.Abs).then_inc(s["absd"], 1)
                if k := at(j, q, 0):
                    b, p, _ = k
                    wait(act, "dl_done", b + 1)
                    act.activation(RS[:, p], ls[:, p, 1:3], ACT.Exp).then_inc(s["exp2_done"], 1)
                if k := at(j, q, 1):
                    b, p, _ = k
                    wait(act, "absd", b + 1)
                    act.activation(L[:, p], L[:, p], ACT.Exp, scale=-1.0).then_inc(s["expd"], 1)
                    wait(act, "expd", b + 1)
                    act.activation(L[:, p], L[:, p], ACT.Ln, bias=1.0).then_inc(s["lnd"], 1)
                if k := at(j, q, -1):
                    b, p, _ = k
                    wait(act, "x2T_ready", b + 1)
                    wait(act, "lg_ready", b - 1)
                    act.activation(xn2T[:, p], T1[:], ACT.Copy).then_inc(s["x2T_sb"], 1)
                if k := at(j, q, 2):
                    b, p, _ = k
                    wait(act, "xT_ready", b + 1)
                    wait(act, "gates_done", b - 1)
                    act.activation(xnT[:, p], T1[:], ACT.Copy).then_inc(s["xT_sb"], 1)

            copy_WT()
            blocks(act, step)

            def xgT_copy(j, k):
                n = RING * j + k
                wait(act, "xgT_ready", n + 1)
                wait(act, "up_done", n - 1)
                act.activation(xgT[:, k % 2], PXT[:, 0:P], ACT.Copy).then_inc(s["xgT_sb"], 1)

            def gelu(j, k):
                n = RING * j + k
                wait(act, "up_done", n + 1)
                wait(act, "hT_ready", n - 1)
                act.activation(hid[:, k % 2], PU, ACT.Gelu).then_inc(s["gelu_done"], 1)

            def body(j, k0, k1):
                for k in range(k0, k1):
                    gelu(j, k)
                    if exists(RING * j + k + 2):
                        xgT_copy(j + (k + 2) // RING, (k + 2) % RING)
            xgT_copy(0, 0)
            xgT_copy(0, 1)
            slots(act, body)

        @block.vector
        def _(dve):
            dve.memset(scan_ones[:], 1.0)
            dve.memset(ones[:], 1.0).then_inc(s["const_dve"], 1)

            def stats(q, src, st, done):
                for t in range(BT):
                    ins = dve.bn_stats(st[:, q, t], src(t))
                ins.then_inc(s[done], 1)

            def normalize(b, q, src, dst, mv, r, rstd_done, done):
                wait(dve, rstd_done, b + 1)
                for t in range(BT):
                    ins = dve.tensor_scalar(dst(t), src(t), mv[:, q, t, 0:1], r[:, q, t:t + 1], ALU.subtract, ALU.mult)
                ins.then_inc(s[done], 1)

            def x_tile(b, t):
                return x[:, bass.ds(b * BT + t, 1), :].rearrange("p a d -> p (a d)")

            def step(j, q):
                if k := at(j, q, 0):
                    b, p, _ = k
                    wait(dve, "lnd", b + 1)
                    dve.scalar_tensor_tensor(ls[:, p].rearrange("p g n -> p (g n)"),
                                             gates[p][:].rearrange("p g n -> p (g n)"), 0.0,
                                             L[:, p].rearrange("p g n -> p (g n)"), ALU.min, ALU.subtract).then_inc(s["ls_done"], 1)
                if k := at(j, q, -1):
                    b, p, jj = k
                    wait(dve, "hb_ready", b + 1)
                    wait(dve, rows_stored[p], 16 * jj)
                    dve.tensor_tensor(x2n[:, p, :, 0:D], x[:, bass.ds(b * BT, BT), :],
                                      T2[:].rearrange("p (t d) -> p t d", t=BT), ALU.add).then_inc(s["x2_done"], 1)
                    wait(dve, "x2_done", b + 1)
                    stats(p, lambda t: x2n[:, p, t, 0:D], st2, "stats2")
                if k := at(j, q, 2):
                    b, p, jj = k
                    wait(dve, x_loaded[p], 16 * (jj + 1))
                    stats(p, lambda t: x_tile(b, t), st1, "stats1")
                if k := at(j, q, 0):
                    b, p, _ = k
                    wait(dve, "exp2_done", b + 1)
                    dve.tensor_scalar(den[:, p], RS[:, p, 0], BIG, 1.0, ALU.min, ALU.add).then_inc(s["den_done"], 1)
                    wait(dve, "den_done", b + 1)
                    dve.reciprocal(Fg[:, p], den[:, p]).then_inc(s["F_done"], 1)
                    wait(dve, "F_done", b + 1)
                    dve.scalar_tensor_tensor(Ig[:, p], RS[:, p, 0], BIG, Fg[:, p], ALU.min, ALU.mult).then_inc(s["I_done"], 1)
                if k := at(j, q, -1):
                    b, p, _ = k
                    normalize(b, p, lambda t: x2n[:, p, t, 0:D], lambda t: x2n[:, p, t, D:2 * D], mv2, rstd2, "rstd2_done", "norm2")
                if k := at(j, q, 2):
                    b, p, _ = k
                    wait(dve, "xT_ready", b - 1)
                    normalize(b, p, lambda t: x_tile(b, t), lambda t: xn[:, p, t], mv1, rstd1, "rstd1_done", "norm1")
                if k := at(j, q, 0):
                    b, p, _ = k
                    wait(dve, "v_done", b + 1)
                    for n in range(N // S):
                        c = slice(n * S, (n + 1) * S)
                        ins = dve.tensor_tensor_scan(h[:, p, c], Fg[:, p, c], val[:, p, c], 0.0, ALU.mult, ALU.add)
                    ins.then_inc(s["scan_done"], 1)
                if k := at(j, q, -1):
                    b, p, _ = k
                    wait(dve, "lg_ready", b + 1)
                    dve.tensor_copy(lg[:, bass.ds(b * BT, BT), :],
                                    T2[:, 0:BT * E].rearrange("p (t e) -> p t e", t=BT)).then_inc(s["lg_sb"], 1)

            blocks(dve, step)

            done = [0]

            def after(ins):
                done[0] += 1
                ins.then_inc(s["route"], 1)
                dve.wait_ge(s["route"], done[0])

            def over_e(ap):
                return ap.unsqueeze(2).to_broadcast([P, NT, E])

            dve.wait_ge(s["const_row"], 11)
            dve.wait_ge(s["lg_sb"], NB)
            after(dve.tensor_reduce(best[:], lg[:], AX.X, ALU.max))
            after(dve.tensor_tensor(tied[:], lg[:], over_e(best[:]), ALU.is_equal))
            after(dve.tensor_tensor(pref[:], tied[:], prefer_first[:].unsqueeze(1).to_broadcast([P, NT, E]), ALU.mult))
            after(dve.tensor_reduce(bestp[:], pref[:], AX.X, ALU.max))
            after(dve.tensor_tensor(O[:], pref[:], over_e(bestp[:]), ALU.is_equal))
            dve.wait_ge(s["counts_ready"], 1)
            after(dve.tensor_copy(tot[:], PI[:, 0:NT * E].rearrange("p (t e) -> p t e", t=NT)))
            for e in range(E):
                ins = dve.tensor_tensor_scan(cum[:, :, e], scan_ones[:], tot[:, :, e], 0.0, ALU.mult, ALU.add)
            after(ins)
            dve.tensor_scalar(nt_i[:], cum[:, NT - 1, :], float(P - 1), None, ALU.add)
            after(dve.tensor_tensor(excl[:], cum[:], tot[:], ALU.subtract))
            dve.tensor_scalar(nt_sh[:], nt_i[:], 7, None, ALU.arith_shift_right)
            after(dve.tensor_tensor(rank3[:], PR[:, 0:NT * E].rearrange("p (t e) -> p t e", t=NT), excl[:], ALU.add))
            dve.tensor_copy(nt_f[:], nt_sh[:])
            after(dve.tensor_tensor(sel[:], rank3[:], O[:], ALU.mult))
            dve.tensor_tensor_scan(cs[:], scan_ones[:, 0:E], nt_f[:], 0.0, ALU.mult, ALU.add)
            with nc.allow_low_precision("whole numbers below 2**24"):
                after(dve.tensor_reduce(rank_i[:], sel[:], AX.X, ALU.add))
            dve.tensor_tensor(base[:], cs[:], nt_f[:], ALU.subtract)
            after(dve.tensor_scalar(rmod_i[:], rank_i[:], P - 1, None, ALU.bitwise_and))
            dve.tensor_copy(rmod[:], rmod_i[:])
            after(dve.tensor_scalar(rdiv_i[:], rank_i[:], 7, None, ALU.arith_shift_right))
            after(dve.tensor_tensor(sbase[:], O[:], base[:].unsqueeze(1).to_broadcast([P, NT, E]), ALU.mult))
            after(dve.tensor_reduce(slot0[:], sbase[:], AX.X, ALU.add))
            after(dve.tensor_tensor(slot[:], slot0[:], rdiv_i[:], ALU.add))
            dve.tensor_tensor(past[:], cs[0:1, :].unsqueeze(1).to_broadcast([1, NS, E]),
                              slot_no[0:1, :].unsqueeze(2).to_broadcast([1, NS, E]), ALU.is_le)
            after(dve.tensor_tensor(S1[:], slot_no[:].unsqueeze(1).to_broadcast([P, NT, NS]),
                                    slot[:].unsqueeze(2).to_broadcast([P, NT, NS]), ALU.is_equal))
            after(dve.tensor_reduce(eid_f[:], past[:], AX.X, ALU.add))
            dve.tensor_tensor(SM[:, :, 0], S1[:], tile_shifted[:].unsqueeze(2).to_broadcast([P, NT, NS]), ALU.mult)
            dve.tensor_scalar(SM[:, :, 1], S1[:], part_no[:, 0:1], None, ALU.mult).then_inc(s["SM_done"], 1)
            dve.tensor_scalar(eid[:], eid_f[:], float(E - 1), float(F), ALU.min, ALU.mult).then_inc(s["slots_done"], 1)
            with dve.Fori(0, NT // BT) as j:
                for t in range(BT):
                    n = j * BT + t
                    dve.tensor_scalar(OJ[:, bass.ds(n, 1), :].rearrange("p a r -> p (a r)"), row_no[:],
                                      rmod[:, bass.ds(n, 1)], None, ALU.is_equal).then_inc(s["OJ_done"], 1)
            dve.wait_ge(s["ids_ready"], 1)
            after(dve.tensor_scalar(low[:], PR[:, NS:2 * NS], float(NO_TOKEN), None, ALU.add))
            dve.scalar_tensor_tensor(ids[:], PR[:, 0:NS], float(P), low[:], ALU.mult, ALU.add).then_inc(s["ids_done"], 1)

            def body(j, k0, k1):
                for k in range(k0, k1):
                    n = RING * j + k
                    wait(dve, "hT_ready", n + 1)
                    wait(dve, "y_ready", n - 1)
                    dve.tensor_copy(hidT[:, k % 2], PHT).then_inc(s["hT_sb"], 1)
                    add(j + (k - 1) // RING, (k - 1) % RING)

            def add(j, k):
                n = RING * j + k
                if not exists(n):
                    return
                wait(dve, "y_ready", n + 1)
                wait(dve, gathered[k], 16 * (j + 1))
                wait(dve, scattered[k], 16 * j)
                dve.tensor_tensor(yo[k][:], PY[:, 0:D], xg[k][:, 0:D], ALU.add).then_inc(s["y_done"], 1)

            slots(dve, body)
            add((NS - 1) // RING, (NS - 1) % RING)

        @block.tensor
        def _(pe):
            pe.wait_ge(s["const_row"], 1)
            pe.wait_ge(s["W_loaded"], 16)
            pe.wait_ge(s["gw_loaded"], 16)
            for g in range(3):
                pe.transpose(T1[:, g * H:(g + 1) * H], W_nat[:, g, :], ident[:])
            pe.transpose(T1[:, 3 * H:3 * H + E], gw_nat[:], ident[0:E, 0:E]).then_inc(s["WT_ready"], 1)
            pe.wait_ge(s["WT_sb"], 1)

            def step(j, q):
                if k := at(j, q, -1):
                    b, p, _ = k
                    wait(pe, "scan_done", b + 1)
                    wait(pe, "lg_sb", b)
                    for t in range(BT):
                        ins = pe.transpose(T2[:, t * D:(t + 1) * D], h[:, p, t * P:(t + 1) * P], ident[:])
                    ins.then_inc(s["hb_ready"], 1)
                if k := at(j, q, 1):
                    b, p, _ = k
                    wait(pe, "xT_sb", b + 1)
                    wait(pe, "ls_done", b - 1)
                    for g in range(3):
                        ins = pe.matmul(gates[p][:, g, :], WT[:, g, :], xnT[:, p], start=True, stop=True)
                    ins.then_inc(s["gates_done"], 1)
                if k := at(j, q, -1):
                    b, p, _ = k
                    wait(pe, "norm2", b + 1)
                    wait(pe, "xT_sb", NB if type(b) is int and b + 2 >= NB else b + 3)
                    for t in range(BT):
                        ins = pe.transpose(T1[:, t * P:(t + 1) * P], x2n[:, p, t, D:2 * D], ident[:])
                    ins.then_inc(s["x2T_ready"], 1)
                if k := at(j, q, 2):
                    b, p, _ = k
                    wait(pe, "norm1", b + 1)
                    wait(pe, "x2T_sb", b - 2)
                    wait(pe, "xT_sb", b)
                    for t in range(BT):
                        ins = pe.transpose(T1[:, t * P:(t + 1) * P], xn[:, p, t], ident[:])
                    ins.then_inc(s["xT_ready"], 1)
                if k := at(j, q, -1):
                    b, p, _ = k
                    wait(pe, "x2T_sb", b + 1)
                    wait(pe, "x2_done", b + 1)
                    for t in range(BT):
                        ins = pe.matmul(T2[:, t * E:(t + 1) * E], xn2T[:, p, t * P:(t + 1) * P], gwT[:], start=True, stop=True)
                    ins.then_inc(s["lg_ready"], 1)

            blocks(pe, step)

            pe.wait_ge(s["const_dve"], 1)
            pe.wait_ge(s["route"], 5)
            pe.matmul(PR[:, 0:NT * E], before[:], O[:].rearrange("p t e -> p (t e)"), start=True, stop=True)
            pe.matmul(PI[:, 0:NT * E], ones[:], O[:].rearrange("p t e -> p (t e)"), start=True, stop=True).then_inc(s["counts_ready"], 1)
            pe.wait_ge(s["SM_done"], 1)
            for t in range(NT):
                pe.wait_ge(s["OJ_done"], t + 1)
                ins = pe.matmul(PR[:, 0:2 * NS], OJ[:, t, :], SM[:, t].rearrange("p a s -> p (a s)"),
                                start=(t == 0), stop=(t == NT - 1))
            ins.then_inc(s["ids_ready"], 1)

            pe.wait_ge(s["slots_done"], 1)
            pe.wait_ge(s["w1_loaded"], 16)
            pe.wait_ge(s["w2_loaded"], 16)

            def expert(n):
                return pe.value_load(eid[0:1, bass.ds(n, 1)], min_val=0, max_val=(E - 1) * F)

            def turn_x(j, k):
                wait(pe, gathered[k], 16 * (j + 1))
                wait(pe, "xgT_sb", RING * j + k)
                pe.transpose(PXT[:, 0:P], xg[k][:, D:2 * D], ident[:]).then_inc(s["xgT_ready"], 1)

            def up(j, k):
                n = RING * j + k
                w = expert(n)
                wait(pe, "xgT_sb", n + 1)
                wait(pe, "gelu_done", n)
                pe.matmul(PU, xgT[:, k % 2], w1[:, bass.ds(w, F)], start=True, stop=True).then_inc(s["up_done"], 1)

            def turn_h(j, k):
                n = RING * j + k
                wait(pe, "gelu_done", n + 1)
                wait(pe, "hT_sb", n)
                for c in range(FC):
                    ins = pe.transpose(PHT[:, c * P:(c + 1) * P], hid[:, k % 2, c * P:(c + 1) * P], ident[:])
                ins.then_inc(s["hT_ready"], 1)

            def down(j, k):
                n = RING * j + k
                w = expert(n)
                wait(pe, "hT_sb", n + 1)
                wait(pe, "y_done", n)
                for c in range(FC):
                    ins = pe.matmul(PY[:, 0:D], hidT[:, k % 2, c * P:(c + 1) * P], w2[:, bass.ds(w + c * D, D)],
                                    start=(c == 0), stop=(c == FC - 1))
                ins.then_inc(s["y_ready"], 1)

            def body(j, k0, k1):
                for k in range(k0, k1):
                    turn_h(j, k)
                    if exists(RING * j + k + 1):
                        up(j + (k + 1) // RING, (k + 1) % RING)
                    if exists(RING * j + k + 2):
                        turn_x(j + (k + 2) // RING, (k + 2) % RING)
                    down(j, k)

            turn_x(0, 0)
            up(0, 0)
            turn_x(0, 1)
            slots(pe, body)


_INS = ["L0_attn_x_t", "L0_attn_W", "L0_ffn_gate_w", "L0_ffn_w1", "L0_ffn_w2"]


def kernel(**inputs):
    import numpy as _np
    import concourse.bacc as _bacc
    from concourse import mybir as _mybir
    from concourse.bass_utils import run_bass_kernel_spmd as _run

    nc = _bacc.Bacc("TRN2", target_bir_lowering=False, num_devices=1)
    arrays, args = {}, []
    for name in _INS:
        a = _np.ascontiguousarray(inputs[name])
        arrays[f"in_{name}_dram"] = a
        args.append(nc.dram_tensor(f"in_{name}_dram", a.shape, _mybir.dt.from_np(a.dtype), kind="ExternalInput").ap())
    args.append(nc.dram_tensor("out_0_dram", inputs["L0_attn_x_t"].shape, _mybir.dt.float32, kind="ExternalOutput").ap())
    build_gru_and_routed_ffn(nc, *args)
    r = _run(nc, [arrays], core_ids=[0])
    return r.results[0]["out_0_dram"]
```

```python
import concourse.bass as bass
from concourse import mybir
from contextlib import ExitStack


def build_gru_and_routed_ffn(nc, x_in, W_in, gate_w_in, w1_in, w2_in, out):
    f32, bf16, i32 = mybir.dt.float32, mybir.dt.bfloat16, mybir.dt.int32
    ALU, ACT, AX = mybir.AluOpType, mybir.ActivationFunctionType, mybir.AxisListType
    P = 128
    B, S, D = x_in.shape
    H = W_in.shape[0] // 3
    E, _, F = w1_in.shape
    T = B * S
    NT = T // P
    BT = 4
    N = BT * P
    NB = NT // BT
    FC = F // P
    NS = NT + E - 1
    GROUP = 3
    RING = 3 * GROUP
    REGION = T + P
    NO_TOKEN = 2 * T
    LN_EPS, EPS = 1e-5, 1e-8

    x_tiles = x_in.rearrange("b s d -> (b s) d").rearrange("(n p) d -> p n d", p=P)
    out_rows = out.rearrange("b s d -> (b s) d")
    rows = nc.dram_tensor("rows_by_expert", (E * REGION, D + 1), f32, kind="Internal").ap()

    ctx = ExitStack()
    with ctx:
        def sb(name, shape, dt=f32):
            return ctx.enter_context(nc.sbuf_tensor(name, shape, dt))

        def sem(name):
            return ctx.enter_context(nc.semaphore(name))

        ident = sb("ident", [P, P])
        ones = sb("ones", [P, P], bf16)
        before = sb("before", [P, P], bf16)
        neg_half = sb("neg_half", [P, BT])
        ln_eps = sb("ln_eps", [P, BT])
        eps = sb("eps", [P, 1])
        scan_ones = sb("scan_ones", [P, E])
        prefer_first = sb("prefer_first", [P, E])
        region_at = sb("region_at", [P, E])
        slot_no = sb("slot_no", [1, NS])
        filler = sb("filler", [P, D + 1])
        W_nat = sb("W_nat", [P, 3, D])
        WT = sb("WT", [P, 3, H])
        gw_nat = sb("gw_nat", [E, D])
        gw_sum = sb("gw_sum", [E, 1])
        gw_mean = sb("gw_mean", [E, 1])
        gw_cen = sb("gw_cen", [E, D])
        gwT = sb("gwT", [P, E])
        w1 = sb("w1", [P, E * F])
        w1h = sb("w1h", [P, E * F], bf16)
        w1l = sb("w1l", [P, E * F], bf16)
        w2 = sb("w2", [P, E * FC * D])
        x = sb("x", [P, NT, D])
        row = sb("row", [P, NT, D + 1])
        st = sb("st", [P, 2, BT, 6])
        mv = sb("mv", [P, 2, BT, 2])
        ve = sb("ve", [P, 2, BT])
        rstd = sb("rstd", [P, 2, BT])
        xn = sb("xn", [P, 2, BT, D])
        xnT = sb("xnT", [P, 2, N])
        x2T = sb("x2T", [P, 2, N])
        L = sb("L", [P, 2, 3, N])
        G = sb("G", [P, 2, N])
        ls = sb("ls", [P, 2, 3, N])
        nd = sb("nd", [P, 2, N])
        sp = sb("sp", [P, 2, N])
        FS = sb("FS", [P, 2, 2, N])
        val = sb("val", [P, 2, N])
        h = sb("h", [P, 2, N])
        best = sb("best", [P, BT])
        tied = sb("tied", [P, BT, E])
        pref = sb("pref", [P, BT, E])
        bestp = sb("bestp", [P, BT])
        O = sb("O", [P, 2, BT, E], bf16)
        Osum = sb("Osum", [P, E])
        run = sb("run", [P, NB + 1, E], bf16)
        placed = sb("placed", [P, BT, E])
        sel = sb("sel", [P, BT, E])
        place = sb("place", [P, 2, BT], i32)
        n_f = sb("n_f", [1, E])
        n_up = sb("n_up", [1, E], i32)
        nt_i = sb("nt_i", [1, E], i32)
        nt = sb("nt", [1, E])
        cs = sb("cs", [1, E])
        fill_f = sb("fill_f", [1, E])
        fill_at = sb("fill_at", [1, E], i32)
        past = sb("past", [1, NS, E])
        past_nt = sb("past_nt", [1, NS, E])
        e_of = sb("e_of", [1, NS])
        base = sb("base", [1, NS])
        in_e = sb("in_e", [1, NS])
        e_row = sb("e_row", [1, NS])
        at_f = sb("at_f", [1, NS])
        slot_at = sb("slot_at", [1, NS], i32)
        slot_w = sb("slot_w", [1, NS], i32)
        xg = [sb(f"xg{k}", [P, D + 1]) for k in range(RING)]
        st2 = sb("st2", [P, RING, 6])
        mv2 = sb("mv2", [P, RING, 2])
        ve2 = sb("ve2", [P, RING])
        rstd2 = sb("rstd2", [P, RING])
        xn2 = sb("xn2", [P, 3, D])
        xh = sb("xh", [P, 3, P], bf16)
        xl = sb("xl", [P, 3, P], bf16)
        hid = sb("hid", [P, 3, F])
        yo = [sb(f"yo{k}", [P, D]) for k in range(RING)]

        T1 = ctx.enter_context(nc.psum_tensor("T1", [P, 512], f32))
        T2 = ctx.enter_context(nc.psum_tensor("T2", [P, 512], f32))
        gates = [ctx.enter_context(nc.psum_tensor(f"gates{k}", [P, 3, N], f32)) for k in range(2)]
        PU = [gates[0][:, k, :] for k in range(3)]
        PY = [gates[1][:, k, 0:D] for k in range(3)]
        PX = T1[:, 0:P]

        names = """ident_zero ident_done before_one before_done pool_consts dve_consts W_loaded gw_loaded w1_loaded
        w2_loaded gw_steps gw_centred WT_ready WT_sb stats ve_done rstd_done norm xT_ready xT_sb gates_done absd expd
        lnd ls_done nd_done ad_done spe_done sp_done logF_done F_done g_done v_done scan_done hb_ready x2_done
        x2T_ready x2T_sb lg_ready route onehot run_done rank_ready place_done w1h_done w1l_done
        n_ready table fillers_ready slots_ready fillers_stored stats2 aggr2 ve2_done rstd2_done norm2 xg_turned
        xh_done xl_done up_done gelu_done down_done y_done""".split()
        s = {n: sem(n) for n in names}
        x_loaded = [sem(f"x_loaded{b}") for b in range(NB)]
        rows_scattered = [sem(f"rows_scattered{q}") for q in range(2)]
        rows_loaded = [sem(f"rows_loaded{k}") for k in range(RING)]
        scattered = [sem(f"scattered{k}") for k in range(RING)]

        def wait(eng, name, value):
            if type(value) is not int or value > 0:
                eng.wait_ge(s[name] if type(name) is str else name, value)

        def is_block(b):
            return 0 <= b < NB

        STEPS = range(-3, NB + 3)

        def is_slot(n):
            return type(n) is not int or 0 <= n < NS

        def slots(eng, body):
            for k in range(-3, RING):
                body(0, k)
            with eng.Fori(1, NS // RING - 1) as j:
                for k in range(RING):
                    body(j, k)
            for n in range((NS // RING - 1) * RING, NS + 1):
                body(n // RING, n % RING)

        def slot(j, k):
            return RING * j + k, k % RING, j + k // RING

        block = ctx.enter_context(nc.Block())

        @block.sync
        def _(sp):
            sp.dma_start(x[:, 0:BT, :], x_tiles[:, 0:BT, :]).then_inc(x_loaded[0], 16)
            sp.dma_start(W_nat[:], W_in.rearrange("(g p) d -> p g d", p=P)).then_inc(s["W_loaded"], 16)
            sp.dma_start(gw_nat[:], gate_w_in).then_inc(s["gw_loaded"], 16)
            for b in range(1, NB):
                sp.dma_start(x[:, b * BT:(b + 1) * BT, :], x_tiles[:, b * BT:(b + 1) * BT, :]).then_inc(x_loaded[b], 16)
            sp.dma_start(w1[:].rearrange("p (e f) -> p e f", e=E), w1_in.rearrange("e d f -> d e f")).then_inc(s["w1_loaded"], 16)
            sp.dma_start(w2[:].rearrange("p (e c d) -> p e c d", e=E, c=FC),
                         w2_in.rearrange("e (c p) d -> p e c d", p=P)).then_inc(s["w2_loaded"], 16)

            sp.wait_ge(s["fillers_ready"], 1)
            for e in range(E):
                at = sp.value_load(fill_at[0:1, e:e + 1], min_val=e * REGION, max_val=e * REGION + T)
                sp.dma_start(rows[bass.ds(at, P), :], filler[:]).then_inc(s["fillers_stored"], 16)
            sp.wait_ge(s["slots_ready"], 1)
            sp.wait_ge(s["fillers_stored"], 16 * E)
            for q in range(2):
                sp.wait_ge(rows_scattered[q], 16 * NT // 2)

            for n in range(NS):
                r = n % RING
                at = sp.value_load(slot_at[0:1, n:n + 1], min_val=0, max_val=E * REGION - P)
                wait(sp, scattered[r], 16 * (n // RING))
                sp.dma_start(xg[r][:], rows[bass.ds(at, P), :]).then_inc(rows_loaded[r], 16)

        @block.gpsimd
        def _(pool):
            pool.memset(ident[:], 0.0).then_inc(s["ident_zero"], 1)
            pool.memset(before[:], 1.0).then_inc(s["before_one"], 1)
            pool.memset(neg_half[:], -0.5)
            pool.memset(ln_eps[:], LN_EPS)
            pool.memset(filler[:], 0.0)
            pool.wait_ge(s["ident_zero"], 1)
            pool.affine_select(out=ident[:], in_=ident[:], compare_op=ALU.not_equal, fill=1.0, base=0,
                               pattern=[[-1, P]], channel_multiplier=1).then_inc(s["ident_done"], 1)
            pool.iota(prefer_first[:], [[-1, E]], base=E, channel_multiplier=0, allow_small_or_imprecise_dtypes=True)
            pool.iota(region_at[:], [[REGION, E]], base=0, channel_multiplier=0, allow_small_or_imprecise_dtypes=True)
            pool.iota(slot_no[:], [[1, NS]], base=0, channel_multiplier=0, allow_small_or_imprecise_dtypes=True)
            pool.iota(row[:, :, D:D + 1].rearrange("p t a -> p (t a)").bitcast(i32), [[P, NT]], base=0, channel_multiplier=1)
            pool.wait_ge(s["before_one"], 1)
            pool.affine_select(out=before[:], in_=before[:], compare_op=ALU.is_gt, fill=0.0, base=0,
                               pattern=[[1, P]], channel_multiplier=-1).then_inc(s["pool_consts"], 1)
            pool.wait_ge(s["pool_consts"], 1)
            pool.iota(filler[:, D:D + 1].bitcast(i32), [[0, 1]], base=NO_TOKEN, channel_multiplier=0).then_inc(s["pool_consts"], 1)
            last_row = pool.to_reg(E * REGION - 1)
            last_token = pool.to_reg(T - 1)

            def scatter_rows(b, t0, t1):
                for t in range(t0, t1):
                    pool.indirect_dma_start(rows, bass.IndirectOffsetOnAxis(place[:, b % 2, t:t + 1], 0), row[:, b * BT + t, :],
                                            None, bounds_check=last_row, oob_is_err=False).then_inc(rows_scattered[b % 2], 16)

            for i in STEPS:
                if is_block(b := i - 1):
                    wait(pool, "F_done", b + 1)
                    pool.tensor_tensor(G[:, b % 2], G[:, b % 2], FS[:, b % 2, 1], ALU.add).then_inc(s["g_done"], 1)
                if is_block(b := i):
                    wait(pool, "ls_done", b + 1)
                    wait(pool, "logF_done", b - 1)
                    pool.tensor_tensor(nd[:, b % 2], ls[:, b % 2, 0], ls[:, b % 2, 1], ALU.subtract).then_inc(s["nd_done"], 1)
                if is_block(b := i - 3):
                    wait(pool, "place_done", b + 1)
                    scatter_rows(b, 0, 2)
                if is_block(b := i + 3):
                    q = b % 2
                    wait(pool, "stats", 2 * b + 2)
                    pool.tensor_tensor(ve[:, q], mv[:, q, :, 1], ln_eps[:], ALU.add).then_inc(s["ve_done"], 1)
                    wait(pool, "ve_done", b + 1)
                    pool.tensor_tensor(rstd[:, q], ve[:, q], neg_half[:], ALU.pow).then_inc(s["rstd_done"], 1)
                if is_block(b := i - 3):
                    scatter_rows(b, 2, BT)

            def rstd_of_group(g):
                c = slice(g * GROUP % RING, g * GROUP % RING + GROUP)
                wait(pool, "aggr2", g + 1)
                wait(pool, "norm2", (g - 3) * GROUP + GROUP)
                pool.tensor_tensor(ve2[:, c], mv2[:, c, 1], ln_eps[:, 0:GROUP], ALU.add).then_inc(s["ve2_done"], 1)
                wait(pool, "ve2_done", g + 1)
                pool.tensor_tensor(rstd2[:, c], ve2[:, c], neg_half[:, 0:GROUP], ALU.pow).then_inc(s["rstd2_done"], 1)

            rstd_of_group(0)
            rstd_of_group(1)
            for n in range(NS):
                if n % GROUP == 1 and (n + 5) // GROUP * GROUP < NS:
                    rstd_of_group((n + 5) // GROUP)
                r = n % RING
                pool.wait_ge(s["y_done"], n + 1)
                pool.indirect_dma_start(out_rows, bass.IndirectOffsetOnAxis(xg[r][:, D:D + 1].bitcast(i32), 0), yo[r][:],
                                        None, bounds_check=last_token, oob_is_err=False).then_inc(scattered[r], 16)
            for r in range(RING):
                pool.wait_ge(scattered[r], 16 * ((NS - 1 - r) // RING + 1))

        @block.scalar
        def _(act):
            act.preload_act_table_set("natural_log_exp_and_others")
            act.wait_ge(s["WT_ready"], 1)
            act.activation(WT[:].rearrange("p g h -> p (g h)"), T1[:, 0:3 * H], ACT.Copy)
            act.activation(gwT[:], T1[:, 3 * H:3 * H + E], ACT.Copy).then_inc(s["WT_sb"], 1)
            act.wait_ge(s["dve_consts"], 1)

            for i in STEPS:
                if is_block(b := i + 2):
                    wait(act, "xT_ready", b + 1)
                    wait(act, "gates_done", b - 1)
                    act.activation(xnT[:, b % 2], T2[:], ACT.Copy).then_inc(s["xT_sb"], 1)
                if is_block(b := i - 2):
                    wait(act, "x2T_ready", b + 1)
                    wait(act, "lg_ready", b - 1)
                    act.activation(x2T[:, b % 2], T1[:], ACT.Copy).then_inc(s["x2T_sb"], 1)
                if is_block(b := i + 1):
                    q = b % 2
                    wait(act, "gates_done", b + 1)
                    wait(act, "v_done", b - 1)
                    wait(act, "ls_done", b - 1)
                    act.activation(G[:, q], gates[q][:, 2, :], ACT.Relu)
                    act.activation(L[:, q, 2], gates[q][:, 2, :], ACT.Relu, scale=-1.0)
                    act.activation(L[:, q, 0:2], gates[q][:, 0:2, :], ACT.Abs).then_inc(s["absd"], 1)
                    wait(act, "absd", b + 1)
                    act.activation(L[:, q], L[:, q], ACT.Exp, scale=-1.0).then_inc(s["expd"], 1)
                if is_block(b := i):
                    q = b % 2
                    wait(act, "ad_done", b + 1)
                    act.activation(sp[:, q], sp[:, q], ACT.Exp, scale=-1.0).then_inc(s["spe_done"], 1)
                    wait(act, "spe_done", b + 1)
                    act.activation(sp[:, q], sp[:, q], ACT.Ln, bias=1.0).then_inc(s["sp_done"], 1)
                if is_block(b := i + 1):
                    q = b % 2
                    wait(act, "expd", b + 1)
                    act.activation(L[:, q], L[:, q], ACT.Ln, bias=1.0).then_inc(s["lnd"], 1)
                if is_block(b := i):
                    q = b % 2
                    wait(act, "logF_done", b + 1)
                    wait(act, "scan_done", b - 1)
                    act.activation(FS[:, q], ls[:, q, 1:3], ACT.Exp, bias=eps[:, 0:1]).then_inc(s["F_done"], 1)
                if i == NB - 1:
                    act.wait_ge(s["w1_loaded"], 16)
                if i >= NB - 1:
                    c = slice((i - NB + 1) * E * F // 4, (i - NB + 2) * E * F // 4)
                    act.activation(w1h[:, c], w1[:, c], ACT.Copy).then_inc(s["w1h_done"], 1)
            act.preload_act_table_set("gelu_and_others")

            def body(j, k):
                n, _, _ = slot(j, k + 1)
                if is_slot(n):
                    wait(act, "up_done", n + 1)
                    wait(act, "down_done", n - 2)
                    act.activation(hid[:, (k + 1) % 3], PU[(k + 1) % 3], ACT.Gelu).then_inc(s["gelu_done"], 1)
                n, _, _ = slot(j, k + 2)
                if is_slot(n):
                    wait(act, "xg_turned", n + 1)
                    wait(act, "up_done", n - 2)
                    act.activation(xh[:, (k + 2) % 3], PX, ACT.Copy).then_inc(s["xh_done"], 1)

            slots(act, body)

        @block.vector
        def _(dve):
            dve.memset(ones[:], 1.0)
            dve.memset(eps[:], EPS)
            dve.memset(scan_ones[:], 1.0)
            dve.memset(run[:, 0], 0.0).then_inc(s["dve_consts"], 1)
            dve.wait_ge(s["gw_loaded"], 16)
            dve.tensor_reduce(gw_sum[:], gw_nat[:], AX.X, ALU.add).then_inc(s["gw_steps"], 1)
            dve.wait_ge(s["gw_steps"], 1)
            dve.tensor_scalar(gw_mean[:], gw_sum[:], 1.0 / D, None, ALU.mult).then_inc(s["gw_steps"], 1)
            dve.wait_ge(s["gw_steps"], 2)
            dve.tensor_scalar(gw_cen[:], gw_nat[:], gw_mean[:, 0:1], None, ALU.subtract).then_inc(s["gw_centred"], 1)

            routed = [0]

            def after(ins):
                routed[0] += 1
                ins.then_inc(s["route"], 1)
                dve.wait_ge(s["route"], routed[0])

            def tiles_of(ap):
                return ap.unsqueeze(1).to_broadcast([P, BT, E])

            def experts_of(ap):
                return ap.unsqueeze(2).to_broadcast([P, BT, E])

            for i in STEPS:
                if is_block(b := i):
                    q = b % 2
                    wait(dve, "lnd", b + 1)
                    dve.scalar_tensor_tensor(ls[:, q].rearrange("p g n -> p (g n)"),
                                             gates[q][:].rearrange("p g n -> p (g n)"), 0.0,
                                             L[:, q].rearrange("p g n -> p (g n)"), ALU.min, ALU.subtract).then_inc(s["ls_done"], 1)
                if is_block(b := i - 1):
                    q = b % 2
                    wait(dve, "g_done", b + 1)
                    dve.scalar_tensor_tensor(val[:, q], FS[:, q, 0], 1.0, G[:, q], ALU.subtract, ALU.mult).then_inc(s["v_done"], 1)
                    wait(dve, "v_done", b + 1)
                    wait(dve, "hb_ready", b - 1)
                    for n in range(N // S):
                        c = slice(n * S, (n + 1) * S)
                        ins = dve.tensor_tensor_scan(h[:, q, c], FS[:, q, 0, c], val[:, q, c], 0.0, ALU.mult, ALU.subtract)
                    ins.then_inc(s["scan_done"], 1)
                if is_block(b := i + 3):
                    wait(dve, x_loaded[b], 16)
                    for t in range(BT):
                        ins = dve.bn_stats(st[:, b % 2, t], x[:, b * BT + t])
                    ins.then_inc(s["stats"], 1)
                if is_block(b := i):
                    wait(dve, "nd_done", b + 1)
                    dve.tensor_scalar(sp[:, b % 2].bitcast(i32), nd[:, b % 2].bitcast(i32), 0x7FFFFFFF, None, ALU.bitwise_and).then_inc(s["ad_done"], 1)
                if is_block(b := i - 2):
                    q = b % 2
                    logits = T1[:, 0:BT * E].rearrange("p (t e) -> p t e", t=BT)
                    wait(dve, "lg_ready", b + 1)
                    after(dve.tensor_reduce(best[:], logits, AX.X, ALU.max))
                    after(dve.tensor_tensor(tied[:], logits, experts_of(best[:]), ALU.is_equal))
                    after(dve.tensor_tensor(pref[:], tied[:], tiles_of(prefer_first[:]), ALU.mult))
                    after(dve.tensor_reduce(bestp[:], pref[:], AX.X, ALU.max))
                    dve.tensor_tensor(O[:, q], pref[:], experts_of(bestp[:]), ALU.is_equal).then_inc(s["onehot"], 1)
                if is_block(b := i + 3):
                    wait(dve, "stats", 2 * b + 1)
                    for t in range(BT):
                        ins = dve.bn_aggr(mv[:, b % 2, t], st[:, b % 2, t])
                    ins.then_inc(s["stats"], 1)
                if is_block(b := i - 1):
                    c = slice(b * BT, (b + 1) * BT)
                    wait(dve, "hb_ready", b + 1)
                    dve.tensor_tensor(row[:, c, 0:D], x[:, c, :], T2[:].rearrange("p (t d) -> p t d", t=BT), ALU.add).then_inc(s["x2_done"], 1)
                if is_block(b := i):
                    q = b % 2
                    wait(dve, "sp_done", b + 1)
                    dve.scalar_tensor_tensor(ls[:, q, 1], nd[:, q], 0.0, sp[:, q], ALU.min, ALU.subtract).then_inc(s["logF_done"], 1)
                if is_block(b := i - 2):
                    q = b % 2
                    wait(dve, "onehot", b + 1)
                    after(dve.tensor_reduce(Osum[:], O[:, q].rearrange("p t e -> p e t"), AX.X, ALU.add))
                    dve.tensor_tensor(run[:, b + 1], run[:, b], Osum[:], ALU.add).then_inc(s["run_done"], 1)
                    wait(dve, "rank_ready", b + 1)
                    after(dve.tensor_tensor(placed[:], T1[:, 64:64 + BT * E].rearrange("p (t e) -> p t e", t=BT),
                                            tiles_of(region_at[:]), ALU.add))
                    after(dve.tensor_tensor(sel[:], placed[:], O[:, q], ALU.mult))
                    wait(dve, rows_scattered[q], 16 * BT * (b // 2))
                    with nc.allow_low_precision("whole numbers below 2**24"):
                        dve.tensor_reduce(place[:, q], sel[:], AX.X, ALU.add).then_inc(s["place_done"], 1)
                if is_block(b := i + 3):
                    q = b % 2
                    wait(dve, "rstd_done", b + 1)
                    wait(dve, "xT_ready", b - 1)
                    for t in range(BT):
                        ins = dve.tensor_scalar(xn[:, q, t], x[:, b * BT + t], mv[:, q, t, 0:1], rstd[:, q, t:t + 1],
                                                ALU.subtract, ALU.mult)
                    ins.then_inc(s["norm"], 1)

            def per_slot(ap):
                return ap.unsqueeze(1).to_broadcast([1, NS, E])

            dve.wait_ge(s["n_ready"], 1)
            after(dve.tensor_copy(n_f[:], T2[0:1, 0:E]))
            dve.tensor_scalar(n_up[:], n_f[:], float(P - 1), None, ALU.add)
            after(dve.tensor_tensor(fill_f[:], n_f[:], region_at[0:1, :], ALU.add))
            dve.tensor_copy(fill_at[:], fill_f[:]).then_inc(s["fillers_ready"], 1)
            after(dve.tensor_scalar(nt_i[:], n_up[:], 7, None, ALU.arith_shift_right))
            after(dve.tensor_copy(nt[:], nt_i[:]))
            after(dve.tensor_tensor_scan(cs[:], scan_ones[0:1, :], nt[:], 0.0, ALU.mult, ALU.add))
            after(dve.tensor_tensor(past[:], per_slot(cs[:]), slot_no[:].unsqueeze(2).to_broadcast([1, NS, E]), ALU.is_le))
            dve.tensor_reduce(e_of[:], past[:], AX.X, ALU.add)
            after(dve.tensor_tensor(past_nt[:], past[:], per_slot(nt[:]), ALU.mult))
            dve.tensor_scalar(e_row[:], e_of[:], float(REGION), None, ALU.mult)
            after(dve.tensor_reduce(base[:], past_nt[:], AX.X, ALU.add))
            dve.tensor_scalar(slot_w[:], e_of[:], float(E - 1), float(F), ALU.min, ALU.mult)
            after(dve.tensor_tensor(in_e[:], slot_no[:], base[:], ALU.subtract))
            after(dve.scalar_tensor_tensor(at_f[:], in_e[:], float(P), e_row[:], ALU.mult, ALU.add))
            dve.tensor_scalar(slot_at[:], at_f[:], fill_f[0:1, E - 1:E], None, ALU.min).then_inc(s["slots_ready"], 1)

            for c in range(4):
                c4 = slice(c * E * F // 4, (c + 1) * E * F // 4)
                dve.wait_ge(s["w1h_done"], c + 1)
                dve.tensor_tensor(w1l[:, c4], w1[:, c4], w1h[:, c4], ALU.subtract).then_inc(s["w1l_done"], 1)

            def stats_of_group(j, k):
                for m in range(k, k + GROUP):
                    n, r, jj = slot(j, m)
                    wait(dve, rows_loaded[r], 16 * (jj + 1))
                    ins = dve.bn_stats(st2[:, r], xg[r][:, 0:D])
                ins.then_inc(s["stats2"], 1)

            def aggregate_group(j, k):
                for m in range(k, k + GROUP):
                    _, r, _ = slot(j, m)
                    ins = dve.bn_aggr(mv2[:, r], st2[:, r])
                ins.then_inc(s["aggr2"], 1)

            def body(j, k):
                n, r, _ = slot(j, k + 3)
                if is_slot(n):
                    wait(dve, "rstd2_done", (RING * j + k) // GROUP + 2 if type(j) is int else (RING // GROUP) * j + k // GROUP + 2)
                    wait(dve, "xg_turned", n - 2)
                    dve.tensor_scalar(xn2[:, r % 3], xg[r][:, 0:D], mv2[:, r, 0:1], rstd2[:, r:r + 1], ALU.subtract, ALU.mult).then_inc(s["norm2"], 1)
                n, r, jj = slot(j, k - 1)
                if is_slot(n):
                    wait(dve, "down_done", n + 1)
                    wait(dve, scattered[r], 16 * jj)
                    dve.tensor_tensor(yo[r][:], PY[r % 3], xg[r][:, 0:D], ALU.add).then_inc(s["y_done"], 1)
                n, _, _ = slot(j, k + 5)
                group = k % GROUP == 1 and is_slot(n)
                g = (RING // GROUP) * j + (k + 5) // GROUP
                if group:
                    stats_of_group(j, k + 5)
                n, r, _ = slot(j, k + 2)
                if is_slot(n):
                    wait(dve, "xh_done", n + 1)
                    if group:
                        wait(dve, "stats2", g + 1)
                    wait(dve, "up_done", n - 2)
                    dve.tensor_tensor(xl[:, r % 3], PX, xh[:, r % 3], ALU.subtract).then_inc(s["xl_done"], 1)
                elif group:
                    wait(dve, "stats2", g + 1)
                if group:
                    aggregate_group(j, k + 5)

            stats_of_group(0, 0)
            dve.wait_ge(s["stats2"], 1)
            aggregate_group(0, 0)
            slots(dve, body)

        @block.tensor
        def _(pe):
            pe.wait_ge(s["ident_done"], 1)
            pe.wait_ge(s["W_loaded"], 16)
            for g in range(3):
                pe.transpose(T1[:, g * H:(g + 1) * H], W_nat[:, g, :], ident[:])
            pe.wait_ge(s["gw_centred"], 1)
            pe.transpose(T1[:, 3 * H:3 * H + E], gw_cen[:], ident[0:E, 0:E]).then_inc(s["WT_ready"], 1)

            for i in STEPS:
                if is_block(b := i - 2):
                    wait(pe, "x2T_sb", b + 1)
                    for t in range(BT):
                        ins = pe.matmul(T1[:, t * E:(t + 1) * E], x2T[:, b % 2, t * P:(t + 1) * P], gwT[:], start=True, stop=True)
                    ins.then_inc(s["lg_ready"], 1)
                if is_block(b := i - 1):
                    wait(pe, "scan_done", b + 1)
                    wait(pe, "xT_sb", min(b + 4, NB))
                    for t in range(BT):
                        ins = pe.transpose(T2[:, t * D:(t + 1) * D], h[:, b % 2, t * P:(t + 1) * P], ident[:])
                    ins.then_inc(s["hb_ready"], 1)
                if is_block(b := i + 2):
                    if b == 0:
                        pe.wait_ge(s["WT_sb"], 1)
                    wait(pe, "xT_sb", b + 1)
                    wait(pe, "ls_done", b - 1)
                    for g in range(3):
                        ins = pe.matmul(gates[b % 2][:, g, :], WT[:, g, :], xnT[:, b % 2], start=True, stop=True)
                    ins.then_inc(s["gates_done"], 1)
                if is_block(b := i - 2):
                    q = b % 2
                    if b == 0:
                        pe.wait_ge(s["pool_consts"], 1)
                        pe.wait_ge(s["dve_consts"], 1)
                    ranks = T1[:, 64:64 + BT * E]
                    wait(pe, "onehot", b + 1)
                    wait(pe, "run_done", b)
                    pe.matmul(ranks, before[:], O[:, q].rearrange("p t e -> p (t e)"), start=True, stop=False)
                    pe.matmul(ranks, ones[:], run[:, b].unsqueeze(1).to_broadcast([P, BT, E]), start=False, stop=False)
                    for t in range(BT - 1):
                        ins = pe.matmul(T1[:, 64 + (t + 1) * E:64 + BT * E], ones[:],
                                        O[:, q, t].unsqueeze(1).to_broadcast([P, BT - 1 - t, E]),
                                        start=False, stop=(t == BT - 2))
                    ins.then_inc(s["rank_ready"], 1)
                if is_block(b := i - 1):
                    wait(pe, "x2_done", b + 1)
                    wait(pe, "place_done", b)
                    for t in range(BT):
                        ins = pe.transpose(T1[:, t * P:(t + 1) * P], row[:, b * BT + t, 0:D], ident[:])
                    ins.then_inc(s["x2T_ready"], 1)
                if is_block(b := i + 3):
                    wait(pe, "norm", b + 1)
                    wait(pe, "x2_done", b - 3)
                    wait(pe, "xT_sb", b)
                    for t in range(BT):
                        ins = pe.transpose(T2[:, t * P:(t + 1) * P], xn[:, b % 2, t], ident[:])
                    ins.then_inc(s["xT_ready"], 1)

            pe.wait_ge(s["run_done"], NB)
            pe.matmul(T2[:, 0:E], ones[:], run[:, NB], start=True, stop=True).then_inc(s["n_ready"], 1)

            pe.wait_ge(s["place_done"], NB)
            pe.wait_ge(s["slots_ready"], 1)
            pe.wait_ge(s["w2_loaded"], 16)
            pe.wait_ge(s["w1l_done"], 4)

            def expert(j, k):
                n, _, _ = slot(j, k)
                return pe.value_load(slot_w[0:1, bass.ds(n, 1)], min_val=0, max_val=(E - 1) * F)

            held = {}

            def body(j, k):
                n, r, _ = slot(j, k + 1)
                if is_slot(n):
                    w = held[r] if r in held and (type(j) is int or k > 0) else expert(j, k + 1)
                    held[r] = w
                    wait(pe, "xh_done", n + 1)
                    wait(pe, "xl_done", n + 1)
                    wait(pe, "gelu_done", n - 2)
                    for c in range(FC):
                        o = PU[r % 3][:, c * P:(c + 1) * P]
                        hi, lo = w1h[:, bass.ds(w + c * P, P)], w1l[:, bass.ds(w + c * P, P)]
                        pe.matmul(o, hi, xh[:, r % 3], start=True, stop=False)
                        pe.matmul(o, hi, xl[:, r % 3], start=False, stop=False)
                        ins = pe.matmul(o, lo, xh[:, r % 3], start=False, stop=True)
                    ins.then_inc(s["up_done"], 1)
                n, r, _ = slot(j, k + 2)
                if is_slot(n):
                    held[r] = expert(j, k + 2)
                    wait(pe, "norm2", n + 1)
                    wait(pe, "xl_done", n)
                    pe.transpose(PX, xn2[:, r % 3], ident[:]).then_inc(s["xg_turned"], 1)
                n, r, _ = slot(j, k)
                if is_slot(n):
                    w = expert(j, k) if type(j) is not int and k == 0 else held[r]
                    wait(pe, "gelu_done", n + 1)
                    wait(pe, "y_done", n - 2)
                    for c in range(FC):
                        ins = pe.matmul(PY[r % 3], hid[:, r % 3, c * P:(c + 1) * P], w2[:, bass.ds(w + c * D, D)],
                                        start=(c == 0), stop=(c == FC - 1))
                    ins.then_inc(s["down_done"], 1)

            slots(pe, body)


_INS = ["L0_attn_x_t", "L0_attn_W", "L0_ffn_gate_w", "L0_ffn_w1", "L0_ffn_w2"]


def kernel(**inputs):
    import numpy as _np
    import concourse.bacc as _bacc
    from concourse import mybir as _mybir
    from concourse.bass_utils import run_bass_kernel_spmd as _run

    nc = _bacc.Bacc("TRN2", target_bir_lowering=False, num_devices=1)
    arrays, args = {}, []
    for name in _INS:
        a = _np.ascontiguousarray(inputs[name])
        arrays[f"in_{name}_dram"] = a
        args.append(nc.dram_tensor(f"in_{name}_dram", a.shape, _mybir.dt.from_np(a.dtype), kind="ExternalInput").ap())
    args.append(nc.dram_tensor("out_0_dram", inputs["L0_attn_x_t"].shape, _mybir.dt.float32, kind="ExternalOutput").ap())
    build_gru_and_routed_ffn(nc, *args)
    r = _run(nc, [arrays], core_ids=[0])
    return r.results[0]["out_0_dram"]
```

```python
import concourse.bass as bass
from concourse import mybir
from contextlib import ExitStack


def build_gru_and_routed_ffn(nc, x_in, W_in, gate_w_in, w1_in, w2_in, out):
    f32, bf16, i32 = mybir.dt.float32, mybir.dt.bfloat16, mybir.dt.int32
    ALU, ACT, AX = mybir.AluOpType, mybir.ActivationFunctionType, mybir.AxisListType
    P = 128
    B, S, D = x_in.shape
    H = W_in.shape[0] // 3
    E, _, F = w1_in.shape
    T = B * S
    NT = T // P
    BT = 4
    N = BT * P
    NB = NT // BT
    FC = F // P
    NS = NT + E - 1
    GROUP = 3
    NG = NS // GROUP
    WARM_UP, KEEP_WARM = 18, (5, 5)
    RING = 6
    REGION = T + P
    NO_TOKEN = 2 * T
    LN_EPS, EPS = 1e-5, 1e-8
    assert REGION % P == 0 and (E - 1) * REGION // P < 256

    x_tiles = x_in.rearrange("b s d -> (b s) d").rearrange("(n p) d -> p n d", p=P)
    out_rows = out.rearrange("b s d -> (b s) d")
    rows = nc.dram_tensor("rows_by_expert", (E * REGION, D + 1), f32, kind="Internal").ap()

    ctx = ExitStack()
    with ctx:
        def sb(name, shape, dt=f32):
            return ctx.enter_context(nc.sbuf_tensor(name, shape, dt))

        def sem(name):
            return ctx.enter_context(nc.semaphore(name))

        ident = sb("ident", [P, P])
        ones = sb("ones", [P, P], bf16)
        before = sb("before", [P, P], bf16)
        neg_half = sb("neg_half", [P, BT])
        ln_eps = sb("ln_eps", [P, BT])
        eps = sb("eps", [P, 1])
        scan_ones = sb("scan_ones", [P, E])
        prefer_first = sb("prefer_first", [P, E])
        region_at = sb("region_at", [P, E])
        region_part = sb("region_part", [P, E], bf16)
        slot_no = sb("slot_no", [1, NS])
        filler = sb("filler", [P, D + 1])
        W_nat = sb("W_nat", [P, 3, D])
        WT = sb("WT", [P, 3, H])
        gw_nat = sb("gw_nat", [E, D])
        gw_sum = sb("gw_sum", [E, 1])
        gw_mean = sb("gw_mean", [E, 1])
        gw_cen = sb("gw_cen", [E, D])
        gwT = sb("gwT", [P, E])
        w1 = sb("w1", [P, E * F])
        w1h = sb("w1h", [P, E * F], bf16)
        w1l = sb("w1l", [P, E * F], bf16)
        w2 = sb("w2", [P, E * FC * D])
        x = sb("x", [P, NT, D])
        row = sb("row", [P, NT, D + 1])
        st = sb("st", [P, 2, BT, 6])
        mv = sb("mv", [P, 2, BT, 2])
        ve = sb("ve", [P, 2, BT])
        rstd = sb("rstd", [P, NB, BT])
        xn = sb("xn", [P, 2, BT, D])
        xnT = sb("xnT", [P, 2, N])
        L = sb("L", [P, 2, 3, N])
        G = sb("G", [P, 2, N])
        ls = sb("ls", [P, 2, 3, N])
        nd = sb("nd", [P, 2, N])
        sp = sb("sp", [P, 2, N])
        FS = sb("FS", [P, 2, 2, N])
        val = sb("val", [P, 2, N])
        h = sb("h", [P, 2, N])
        lg_x = sb("lg_x", [P, NB, BT, E])
        lg_h = sb("lg_h", [P, BT, E])
        lg = sb("lg", [P, BT, E])
        best = sb("best", [P, BT])
        tied = sb("tied", [P, BT, E])
        pref = sb("pref", [P, BT, E])
        bestp = sb("bestp", [P, BT])
        O = sb("O", [P, 2, BT, E], bf16)
        Osum = sb("Osum", [P, E])
        run = sb("run", [P, NB + 1, E], bf16)
        sel = sb("sel", [P, BT, E])
        place = sb("place", [P, 2, BT], i32)
        n_f = sb("n_f", [1, E])
        n_up = sb("n_up", [1, E], i32)
        nt_i = sb("nt_i", [1, E], i32)
        nt = sb("nt", [1, E])
        cs = sb("cs", [1, E])
        fill_f = sb("fill_f", [1, E])
        fill_at = sb("fill_at", [1, E], i32)
        past = sb("past", [1, NS, E])
        past_nt = sb("past_nt", [1, NS, E])
        e_of = sb("e_of", [1, NS])
        base = sb("base", [1, NS])
        in_e = sb("in_e", [1, NS])
        e_row = sb("e_row", [1, NS])
        at_f = sb("at_f", [1, NS])
        slot_at = sb("slot_at", [1, NS], i32)
        slot_w = sb("slot_w", [1, NS], i32)
        xg = [sb(f"xg{n}", [P, D + 1]) for n in range(NS)]
        st2 = sb("st2", [P, NS, 6])
        mv2 = sb("mv2", [P, NS, 2])
        ve2 = sb("ve2", [P, NS])
        rstd2 = sb("rstd2", [P, NS])
        xn2 = sb("xn2", [P, 3, D])
        xh = sb("xh", [P, 3, P], bf16)
        xl = sb("xl", [P, 3, P], bf16)
        hid = sb("hid", [P, 3, F])
        yo = [sb(f"yo{k}", [P, D]) for k in range(RING)]

        T1 = ctx.enter_context(nc.psum_tensor("T1", [P, 512], f32))
        T2 = ctx.enter_context(nc.psum_tensor("T2", [P, 512], f32))
        gates = [ctx.enter_context(nc.psum_tensor(f"gates{k}", [P, 3, N], f32)) for k in range(2)]
        PU = [gates[0][:, k, :] for k in range(3)]
        PY = [gates[1][:, k, 0:D] for k in range(3)]
        PX = [T1[:, 0:P], T2[:, 0:P]]

        names = """ident_zero ident_done before_one pool_consts dve_consts W_loaded gw_loaded w1_loaded
        w2_loaded gw_steps gw_centred WT_ready WT_sb stats ve_done rstd_done norm xT_ready xT_sb gates_done absd expd
        lnd ls_done nd_done ad_done spe_done sp_done logF_done F_done g_done v_done scan_done hb_ready x2_done
        lg_x_ready lg_x_done lg_ready route onehot ranks_used run_done rank_ready place_done w1h_done w1l_done
        n_ready fillers_ready slots_ready fillers_stored stats2 aggr2 ve2_done rstd2_done norm2 xg_turned
        xh_done xl_done up_done gelu_done down_done y_done""".split()
        s = {n: sem(n) for n in names}
        x_loaded = [sem(f"x_loaded{b}") for b in range(NB)]
        rows_scattered = [sem(f"rows_scattered{q}") for q in range(2)]
        rows_loaded = [sem(f"rows_loaded{g}") for g in range(NG)]
        scattered = [sem(f"scattered{k}") for k in range(RING)]

        def wait(eng, name, value):
            if type(value) is not int or value > 0:
                eng.wait_ge(s[name] if type(name) is str else name, value)

        def is_block(b):
            return 0 <= b < NB

        STEPS = range(-3, NB + 2)

        FFN_STEPS = range(-6, NS + 4)

        def is_slot(n):
            return 0 <= n < NS

        block = ctx.enter_context(nc.Block())

        @block.sync
        def _(sp):
            def places(at):
                return nc.values_load_multi_w_load_instructions(
                    at, engines=[mybir.EngineType.SP], min_val=0, max_val=E * REGION - P,
                    skip_runtime_bounds_check_because="counts of T tokens, kept below the last region's end by VectorE")[1]

            sp.dma_start(x[:, 0:BT, :], x_tiles[:, 0:BT, :]).then_inc(x_loaded[0], 16)
            sp.dma_start(W_nat[:], W_in.rearrange("(g p) d -> p g d", p=P)).then_inc(s["W_loaded"], 16)
            sp.dma_start(gw_nat[:], gate_w_in).then_inc(s["gw_loaded"], 16)
            for b in range(1, NB):
                sp.dma_start(x[:, b * BT:(b + 1) * BT, :], x_tiles[:, b * BT:(b + 1) * BT, :]).then_inc(x_loaded[b], 16)
            sp.dma_start(w1[:].rearrange("p (e f) -> p e f", e=E), w1_in.rearrange("e d f -> d e f")).then_inc(s["w1_loaded"], 16)
            sp.dma_start(w2[:].rearrange("p (e c d) -> p e c d", e=E, c=FC),
                         w2_in.rearrange("e (c p) d -> p e c d", p=P)).then_inc(s["w2_loaded"], 16)

            sp.wait_ge(s["fillers_ready"], 1)
            for e, at in enumerate(places(fill_at[0:1, :])):
                sp.dma_start(rows[bass.ds(at, P), :], filler[:]).then_inc(s["fillers_stored"], 16)
            sp.wait_ge(s["slots_ready"], 1)
            next_rows = places(slot_at[0:1, 0:GROUP])
            sp.wait_ge(s["fillers_stored"], 16 * E)
            for q in range(2):
                sp.wait_ge(rows_scattered[q], 16 * NT // 2)

            for g in range(NG):
                for m, at in enumerate(next_rows):
                    sp.dma_start(xg[g * GROUP + m][:], rows[bass.ds(at, P), :]).then_inc(rows_loaded[g], 16)
                if g + 1 < NG:
                    next_rows = places(slot_at[0:1, (g + 1) * GROUP:(g + 2) * GROUP])

        @block.gpsimd
        def _(pool):
            pool.memset(ident[:], 0.0).then_inc(s["ident_zero"], 1)
            pool.memset(before[:], 1.0).then_inc(s["before_one"], 1)
            pool.memset(neg_half[:], -0.5)
            pool.memset(ln_eps[:], LN_EPS)
            pool.memset(filler[:], 0.0)
            pool.wait_ge(s["ident_zero"], 1)
            pool.affine_select(out=ident[:], in_=ident[:], compare_op=ALU.not_equal, fill=1.0, base=0,
                               pattern=[[-1, P]], channel_multiplier=1).then_inc(s["ident_done"], 1)
            pool.iota(prefer_first[:], [[-1, E]], base=E, channel_multiplier=0, allow_small_or_imprecise_dtypes=True)
            pool.iota(region_at[:], [[REGION, E]], base=0, channel_multiplier=0, allow_small_or_imprecise_dtypes=True)
            pool.iota(region_part[:], [[REGION // P, E]], base=0, channel_multiplier=0, allow_small_or_imprecise_dtypes=True)
            pool.iota(slot_no[:], [[1, NS]], base=0, channel_multiplier=0, allow_small_or_imprecise_dtypes=True)
            pool.iota(row[:, :, D:D + 1].rearrange("p t a -> p (t a)").bitcast(i32), [[P, NT]], base=0, channel_multiplier=1)
            pool.wait_ge(s["before_one"], 1)
            pool.affine_select(out=before[:], in_=before[:], compare_op=ALU.is_gt, fill=0.0, base=0,
                               pattern=[[1, P]], channel_multiplier=-1).then_inc(s["pool_consts"], 1)
            pool.wait_ge(s["pool_consts"], 1)
            pool.iota(filler[:, D:D + 1].bitcast(i32), [[0, 1]], base=NO_TOKEN, channel_multiplier=0).then_inc(s["pool_consts"], 1)
            last_row = pool.to_reg(E * REGION - 1)
            last_token = pool.to_reg(T - 1)

            def scatter_rows(b, t0, t1):
                for t in range(t0, t1):
                    pool.indirect_dma_start(rows, bass.IndirectOffsetOnAxis(place[:, b % 2, t:t + 1], 0), row[:, b * BT + t, :],
                                            None, bounds_check=last_row, oob_is_err=False).then_inc(rows_scattered[b % 2], 16)

            for i in STEPS:
                if is_block(b := i - 1):
                    wait(pool, "F_done", b + 1)
                    pool.tensor_tensor(G[:, b % 2], G[:, b % 2], FS[:, b % 2, 1], ALU.add).then_inc(s["g_done"], 1)
                if is_block(b := i):
                    wait(pool, "ls_done", b + 1)
                    wait(pool, "logF_done", b - 1)
                    pool.tensor_tensor(nd[:, b % 2], ls[:, b % 2, 0], ls[:, b % 2, 1], ALU.subtract).then_inc(s["nd_done"], 1)
                if is_block(b := i - 2):
                    wait(pool, "place_done", b + 1)
                    scatter_rows(b, 0, 1)
                if is_block(b := i + 3):
                    q = b % 2
                    wait(pool, "stats", 2 * b + 2)
                    pool.tensor_tensor(ve[:, q], mv[:, q, :, 1], ln_eps[:], ALU.add).then_inc(s["ve_done"], 1)
                    wait(pool, "ve_done", b + 1)
                    pool.tensor_tensor(rstd[:, b], ve[:, q], neg_half[:], ALU.pow).then_inc(s["rstd_done"], 1)
                if is_block(b := i - 2):
                    scatter_rows(b, 1, BT)

            for n in FFN_STEPS:
                if is_slot(n - 4):
                    r = (n - 4) % RING
                    pool.wait_ge(s["y_done"], n - 3)
                    pool.indirect_dma_start(out_rows, bass.IndirectOffsetOnAxis(xg[n - 4][:, D:D + 1].bitcast(i32), 0), yo[r][:],
                                            None, bounds_check=last_token, oob_is_err=False).then_inc(scattered[r], 16)
                if (n + 6) % GROUP == 0 and is_slot(n + 6):
                    g = (n + 6) // GROUP
                    c = slice(g * GROUP, (g + 1) * GROUP)
                    wait(pool, "aggr2", g + 1)
                    pool.tensor_tensor(ve2[:, c], mv2[:, c, 1], ln_eps[:, 0:GROUP], ALU.add).then_inc(s["ve2_done"], 1)
                    wait(pool, "ve2_done", g + 1)
                    pool.tensor_tensor(rstd2[:, c], ve2[:, c], neg_half[:, 0:GROUP], ALU.pow).then_inc(s["rstd2_done"], 1)
            for r in range(RING):
                pool.wait_ge(scattered[r], 16 * ((NS - 1 - r) // RING + 1))

        @block.scalar
        def _(act):
            act.preload_act_table_set("natural_log_exp_and_others")
            act.wait_ge(s["WT_ready"], 1)
            act.activation(WT[:].rearrange("p g h -> p (g h)"), T1[:, 0:3 * H], ACT.Copy)
            act.activation(gwT[:], T1[:, 3 * H:3 * H + E], ACT.Copy).then_inc(s["WT_sb"], 1)
            act.wait_ge(s["dve_consts"], 1)

            for i in STEPS:
                if is_block(b := i + 1):
                    q = b % 2
                    wait(act, "gates_done", b + 1)
                    wait(act, "ls_done", b - 1)
                    act.activation(L[:, q, 2], gates[q][:, 2, :], ACT.Relu, scale=-1.0)
                if is_block(b := i + 2):
                    wait(act, "xT_ready", b + 1)
                    wait(act, "lg_x_ready", b - 1)
                    act.activation(xnT[:, b % 2], T2[:], ACT.Copy).then_inc(s["xT_sb"], 1)
                if is_block(b := i + 1):
                    q = b % 2
                    act.activation(L[:, q, 0:2], gates[q][:, 0:2, :], ACT.Abs).then_inc(s["absd"], 1)
                    wait(act, "v_done", b - 1)
                    act.activation(G[:, q], gates[q][:, 2, :], ACT.Relu)
                    wait(act, "absd", b + 1)
                    act.activation(L[:, q], L[:, q], ACT.Exp, scale=-1.0).then_inc(s["expd"], 1)
                if is_block(b := i):
                    q = b % 2
                    wait(act, "ad_done", b + 1)
                    act.activation(sp[:, q], sp[:, q], ACT.Exp, scale=-1.0).then_inc(s["spe_done"], 1)
                    wait(act, "spe_done", b + 1)
                    act.activation(sp[:, q], sp[:, q], ACT.Ln, bias=1.0).then_inc(s["sp_done"], 1)
                if is_block(b := i + 1):
                    q = b % 2
                    wait(act, "expd", b + 1)
                    act.activation(L[:, q], L[:, q], ACT.Ln, bias=1.0).then_inc(s["lnd"], 1)
                if is_block(b := i):
                    q = b % 2
                    wait(act, "logF_done", b + 1)
                    wait(act, "scan_done", b - 1)
                    act.activation(FS[:, q], ls[:, q, 1:3], ACT.Exp, bias=eps[:, 0:1]).then_inc(s["F_done"], 1)
                if i == NB - 1:
                    act.wait_ge(s["w1_loaded"], 16)
                if i >= NB - 1:
                    for c in ([0], [1, 2], [3])[i - NB + 1]:
                        c4 = slice(c * E * F // 4, (c + 1) * E * F // 4)
                        act.activation(w1h[:, c4], w1[:, c4], ACT.Copy).then_inc(s["w1h_done"], 1)
            act.preload_act_table_set("gelu_and_others")

            for n in FFN_STEPS:
                if is_slot(n):
                    wait(act, "up_done", n + 1)
                    wait(act, "down_done", n - 2)
                    act.activation(hid[:, n % 3], PU[n % 3], ACT.Gelu).then_inc(s["gelu_done"], 1)
                if is_slot(m := n + 2):
                    wait(act, "xg_turned", m + 1)
                    wait(act, "up_done", m - 2)
                    act.activation(xh[:, m % 3], PX[m % 2], ACT.Copy).then_inc(s["xh_done"], 1)

        @block.vector
        def _(dve):
            dve.memset(ones[:], 1.0)
            dve.memset(eps[:], EPS)
            dve.memset(scan_ones[:], 1.0)
            dve.memset(run[:, 0], 0.0).then_inc(s["dve_consts"], 1)
            routed = [0]

            def after(ins):
                routed[0] += 1
                ins.then_inc(s["route"], 1)
                dve.wait_ge(s["route"], routed[0])

            def tiles_of(ap):
                return ap.unsqueeze(1).to_broadcast([P, BT, E])

            def experts_of(ap):
                return ap.unsqueeze(2).to_broadcast([P, BT, E])

            def link(ins):
                routed[0] += 1
                ins.then_inc(s["route"], 1)

            def linked():
                dve.wait_ge(s["route"], routed[0])

            for i in STEPS:
                a, routing = i - 1, is_block(i - 1)
                if is_block(b := i):
                    q = b % 2
                    wait(dve, "lnd", b + 1)
                    dve.scalar_tensor_tensor(ls[:, q].rearrange("p g n -> p (g n)"),
                                             gates[q][:].rearrange("p g n -> p (g n)"), 0.0,
                                             L[:, q].rearrange("p g n -> p (g n)"), ALU.min, ALU.subtract).then_inc(s["ls_done"], 1)
                if is_block(b := i - 1):
                    q = b % 2
                    wait(dve, "g_done", b + 1)
                    dve.scalar_tensor_tensor(val[:, q], FS[:, q, 0], 1.0, G[:, q], ALU.subtract, ALU.mult).then_inc(s["v_done"], 1)
                if is_block(b := i + 1):
                    wait(dve, "lg_x_ready", b + 1)
                    dve.tensor_copy(lg_x[:, b], T1[:, 0:BT * E].rearrange("p (t e) -> p t e", t=BT)).then_inc(s["lg_x_done"], 1)
                if is_block(b := i - 1):
                    q = b % 2
                    wait(dve, "v_done", b + 1)
                    for n in range(N // S):
                        c = slice(n * S, (n + 1) * S)
                        ins = dve.tensor_tensor_scan(h[:, q, c], FS[:, q, 0, c], val[:, q, c], 0.0, ALU.mult, ALU.subtract)
                    ins.then_inc(s["scan_done"], 1)
                if is_block(b := i + 3):
                    wait(dve, x_loaded[b], 16)
                    for t in range(BT):
                        ins = dve.bn_stats(st[:, b % 2, t], x[:, b * BT + t])
                    ins.then_inc(s["stats"], 1)
                if is_block(b := i):
                    wait(dve, "nd_done", b + 1)
                    dve.tensor_scalar(sp[:, b % 2].bitcast(i32), nd[:, b % 2].bitcast(i32), 0x7FFFFFFF, None, ALU.bitwise_and).then_inc(s["ad_done"], 1)
                if i == STEPS[0]:
                    dve.wait_ge(s["gw_loaded"], 16)
                    dve.tensor_reduce(gw_sum[:], gw_nat[:], AX.X, ALU.add).then_inc(s["gw_steps"], 1)
                    dve.wait_ge(s["gw_steps"], 1)
                    dve.tensor_scalar(gw_mean[:], gw_sum[:], 1.0 / D, None, ALU.mult).then_inc(s["gw_steps"], 1)
                    dve.wait_ge(s["gw_steps"], 2)
                    dve.tensor_scalar(gw_cen[:], gw_nat[:], gw_mean[:, 0:1], None, ALU.subtract).then_inc(s["gw_centred"], 1)
                if is_block(b := i + 3):
                    wait(dve, "stats", 2 * b + 1)
                    for t in range(BT):
                        ins = dve.bn_aggr(mv[:, b % 2, t], st[:, b % 2, t])
                    ins.then_inc(s["stats"], 1)
                if is_block(b := i - 1):
                    c = slice(b * BT, (b + 1) * BT)
                    wait(dve, "hb_ready", b + 1)
                    dve.tensor_tensor(row[:, c, 0:D], x[:, c, :], T1[:].rearrange("p (t d) -> p t d", t=BT), ALU.add).then_inc(s["x2_done"], 1)
                if routing:
                    wait(dve, "lg_ready", a + 1)
                    link(dve.tensor_tensor(lg_h[:], T2[:, BT * E:2 * BT * E].rearrange("p (t e) -> p t e", t=BT),
                                           experts_of(rstd[:, a]), ALU.mult))
                    linked()
                    link(dve.tensor_tensor(lg[:], lg_x[:, a], lg_h[:], ALU.add))
                if is_block(b := i):
                    q = b % 2
                    wait(dve, "sp_done", b + 1)
                    dve.scalar_tensor_tensor(ls[:, q, 1], nd[:, q], 0.0, sp[:, q], ALU.min, ALU.subtract).then_inc(s["logF_done"], 1)
                if routing:
                    linked()
                    link(dve.tensor_reduce(best[:], lg[:], AX.X, ALU.max))
                if is_block(b := i + 3):
                    wait(dve, "rstd_done", b + 1)
                    wait(dve, "xT_ready", b - 1)
                for t in range(BT):
                    if is_block(b := i + 3):
                        ins = dve.tensor_scalar(xn[:, b % 2, t], x[:, b * BT + t], mv[:, b % 2, t, 0:1], rstd[:, b, t:t + 1],
                                                ALU.subtract, ALU.mult)
                        if t == BT - 1:
                            ins.then_inc(s["norm"], 1)
                    if routing and t == 0:
                        linked()
                        link(dve.tensor_tensor(tied[:], lg[:], experts_of(best[:]), ALU.is_equal))
                    if routing and t == 1:
                        linked()
                        link(dve.tensor_tensor(pref[:], tied[:], tiles_of(prefer_first[:]), ALU.mult))
                    if routing and t == 2:
                        linked()
                        link(dve.tensor_reduce(bestp[:], pref[:], AX.X, ALU.max))
                if routing:
                    linked()
                    dve.tensor_tensor(O[:, a % 2], pref[:], experts_of(bestp[:]), ALU.is_equal).then_inc(s["onehot"], 1)
                    wait(dve, "onehot", a + 1)
                    link(dve.tensor_reduce(Osum[:], O[:, a % 2].rearrange("p t e -> p e t"), AX.X, ALU.add))
                    linked()
                    dve.tensor_tensor(run[:, a + 1], run[:, a], Osum[:], ALU.add).then_inc(s["run_done"], 1)
                    wait(dve, "rank_ready", a + 1)
                    dve.tensor_tensor(sel[:], T2[:, 64:64 + BT * E].rearrange("p (t e) -> p t e", t=BT),
                                      O[:, a % 2], ALU.mult).then_inc(s["ranks_used"], 1)
                    wait(dve, "ranks_used", a + 1)
                    wait(dve, rows_scattered[a % 2], 16 * BT * (a // 2))
                    with nc.allow_low_precision("whole numbers below 2**24"):
                        dve.tensor_reduce(place[:, a % 2], sel[:], AX.X, ALU.add).then_inc(s["place_done"], 1)

            def per_slot(ap):
                return ap.unsqueeze(1).to_broadcast([1, NS, E])

            dve.wait_ge(s["n_ready"], 1)
            after(dve.tensor_copy(n_f[:], T1[0:1, 0:E]))
            dve.tensor_scalar(n_up[:], n_f[:], float(P - 1), None, ALU.add)
            after(dve.tensor_tensor(fill_f[:], n_f[:], region_at[0:1, :], ALU.add))
            dve.tensor_copy(fill_at[:], fill_f[:]).then_inc(s["fillers_ready"], 1)
            after(dve.tensor_scalar(nt_i[:], n_up[:], 7, None, ALU.arith_shift_right))
            after(dve.tensor_copy(nt[:], nt_i[:]))
            after(dve.tensor_tensor_scan(cs[:], scan_ones[0:1, :], nt[:], 0.0, ALU.mult, ALU.add))
            after(dve.tensor_tensor(past[:], per_slot(cs[:]), slot_no[:].unsqueeze(2).to_broadcast([1, NS, E]), ALU.is_le))
            dve.tensor_reduce(e_of[:], past[:], AX.X, ALU.add)
            after(dve.tensor_tensor(past_nt[:], past[:], per_slot(nt[:]), ALU.mult))
            dve.tensor_scalar(e_row[:], e_of[:], float(REGION), None, ALU.mult)
            after(dve.tensor_reduce(base[:], past_nt[:], AX.X, ALU.add))
            dve.tensor_scalar(slot_w[:], e_of[:], float(E - 1), float(F), ALU.min, ALU.mult)
            after(dve.tensor_tensor(in_e[:], slot_no[:], base[:], ALU.subtract))
            after(dve.scalar_tensor_tensor(at_f[:], in_e[:], float(P), e_row[:], ALU.mult, ALU.add))
            dve.tensor_scalar(slot_at[:], at_f[:], fill_f[0:1, E - 1:E], None, ALU.min).then_inc(s["slots_ready"], 1)

            for c in range(4):
                c4 = slice(c * E * F // 4, (c + 1) * E * F // 4)
                dve.wait_ge(s["w1h_done"], c + 1)
                dve.tensor_tensor(w1l[:, c4], w1[:, c4], w1h[:, c4], ALU.subtract).then_inc(s["w1l_done"], 1)

            for n in FFN_STEPS:
                if is_slot(m := n - 3):
                    wait(dve, "down_done", m + 1)
                    if m >= RING:
                        dve.wait_ge(scattered[m % RING], 16 * (m // RING))
                    dve.tensor_tensor(yo[m % RING][:], PY[m % 3], xg[m][:, 0:D], ALU.add).then_inc(s["y_done"], 1)
                if is_slot(m := n + 3):
                    wait(dve, "rstd2_done", m // GROUP + 1)
                    wait(dve, "xg_turned", m - 2)
                    dve.tensor_scalar(xn2[:, m % 3], xg[m][:, 0:D], mv2[:, m, 0:1], rstd2[:, m:m + 1], ALU.subtract, ALU.mult).then_inc(s["norm2"], 1)
                first = {-6: 0, -2: GROUP}.get(n, n + 6 if n >= 0 and n % GROUP == 0 else NS)
                group = is_slot(first)
                if group:
                    g = first // GROUP
                    dve.wait_ge(rows_loaded[g], 16 * GROUP)
                    for m in range(first, first + GROUP):
                        ins = dve.bn_stats(st2[:, m], xg[m][:, 0:D])
                    ins.then_inc(s["stats2"], 1)
                if is_slot(m := n + 2):
                    wait(dve, "xh_done", m + 1)
                    wait(dve, "up_done", m - 2)
                    dve.tensor_tensor(xl[:, m % 3], PX[m % 2], xh[:, m % 3], ALU.subtract).then_inc(s["xl_done"], 1)
                if group:
                    dve.wait_ge(s["stats2"], g + 1)
                    for m in range(first, first + GROUP):
                        ins = dve.bn_aggr(mv2[:, m], st2[:, m])
                    ins.then_inc(s["aggr2"], 1)

        @block.tensor
        def _(pe):
            def keep_warm(bank, products):
                for _ in range(products):
                    pe.matmul(bank[:], ones[:], ones[:].unsqueeze(1).to_broadcast([P, BT, P]), start=True, stop=True)

            pe.wait_ge(s["dve_consts"], 1)
            keep_warm(T2, WARM_UP)
            pe.wait_ge(s["ident_done"], 1)
            pe.wait_ge(s["W_loaded"], 16)
            for g in range(3):
                pe.transpose(T1[:, g * H:(g + 1) * H], W_nat[:, g, :], ident[:])
            pe.wait_ge(s["gw_centred"], 1)
            pe.transpose(T1[:, 3 * H:3 * H + E], gw_cen[:], ident[0:E, 0:E]).then_inc(s["WT_ready"], 1)

            for i in STEPS:
                if is_block(b := i + 2):
                    if b == 0:
                        pe.wait_ge(s["WT_sb"], 1)
                    wait(pe, "xT_sb", b + 1)
                    wait(pe, "ls_done", b - 1)
                    pe.matmul(gates[b % 2][:, 0, :], WT[:, 0, :], xnT[:, b % 2], start=True, stop=True)
                if is_block(b := i - 1):
                    wait(pe, "lg_x_done", min(b + 3, NB))
                    wait(pe, "x2_done", b)
                    keep_warm(T1, KEEP_WARM[0])
                    wait(pe, "scan_done", b + 1)
                    for t in range(BT):
                        ins = pe.transpose(T1[:, t * D:(t + 1) * D], h[:, b % 2, t * P:(t + 1) * P], ident[:])
                    ins.then_inc(s["hb_ready"], 1)
                    wait(pe, "xT_sb", min(b + 4, NB))
                    for t in range(BT):
                        ins = pe.matmul(T2[:, (BT + t) * E:(BT + t + 1) * E], h[:, b % 2, t * P:(t + 1) * P], gwT[:], start=True, stop=True)
                    ins.then_inc(s["lg_ready"], 1)
                if is_block(b := i + 2):
                    for g in (1, 2):
                        ins = pe.matmul(gates[b % 2][:, g, :], WT[:, g, :], xnT[:, b % 2], start=True, stop=True)
                    ins.then_inc(s["gates_done"], 1)
                if is_block(b := i - 1):
                    q = b % 2
                    if b == 0:
                        pe.wait_ge(s["pool_consts"], 1)
                        pe.wait_ge(s["dve_consts"], 1)
                    wait(pe, "x2_done", b + 1)
                    keep_warm(T1, KEEP_WARM[1])
                    ranks = T2[:, 64:64 + BT * E]
                    wait(pe, "onehot", b + 1)
                    wait(pe, "run_done", b)
                    pe.matmul(ranks, before[:], O[:, q].rearrange("p t e -> p (t e)"), start=True, stop=False)
                    pe.matmul(ranks, ones[:], run[:, b].unsqueeze(1).to_broadcast([P, BT, E]), start=False, stop=False)
                    pe.matmul(ranks, ones[:], region_part[:].unsqueeze(1).to_broadcast([P, BT, E]), start=False, stop=False)
                    for t in range(BT - 1):
                        ins = pe.matmul(T2[:, 64 + (t + 1) * E:64 + BT * E], ones[:],
                                        O[:, q, t].unsqueeze(1).to_broadcast([P, BT - 1 - t, E]),
                                        start=False, stop=(t == BT - 2))
                    ins.then_inc(s["rank_ready"], 1)
                if is_block(b := i + 3):
                    wait(pe, "norm", b + 1)
                    wait(pe, "xT_sb", b)
                    wait(pe, "ranks_used", b - 3)
                    for t in range(BT):
                        ins = pe.transpose(T2[:, t * P:(t + 1) * P], xn[:, b % 2, t], ident[:])
                    ins.then_inc(s["xT_ready"], 1)
                if is_block(b := i + 2):
                    wait(pe, "x2_done", b - 2)
                    wait(pe, "lg_x_done", b)
                    for t in range(BT):
                        ins = pe.matmul(T1[:, t * E:(t + 1) * E], xnT[:, b % 2, t * P:(t + 1) * P], gwT[:], start=True, stop=True)
                    ins.then_inc(s["lg_x_ready"], 1)

            pe.wait_ge(s["run_done"], NB)
            pe.matmul(T1[:, 0:E], ones[:], run[:, NB], start=True, stop=True).then_inc(s["n_ready"], 1)

            pe.wait_ge(s["place_done"], NB)
            pe.wait_ge(s["slots_ready"], 1)
            pe.wait_ge(s["w2_loaded"], 16)
            pe.wait_ge(s["w1l_done"], 4)

            first_channel = [None] * NS
            for n in FFN_STEPS:
                if is_slot(n):
                    w = first_channel[n]
                    wait(pe, "xl_done", n + 1)
                    for c in range(FC):
                        o = PU[n % 3][:, c * P:(c + 1) * P]
                        hi, lo = w1h[:, bass.ds(w + c * P, P)], w1l[:, bass.ds(w + c * P, P)]
                        pe.matmul(o, hi, xh[:, n % 3], start=True, stop=False)
                        pe.matmul(o, hi, xl[:, n % 3], start=False, stop=False)
                        ins = pe.matmul(o, lo, xh[:, n % 3], start=False, stop=True)
                    ins.then_inc(s["up_done"], 1)
                if is_slot(m := n + 2):
                    wait(pe, "norm2", m + 1)
                    pe.transpose(PX[m % 2], xn2[:, m % 3], ident[:]).then_inc(s["xg_turned"], 1)
                if is_slot(m := n - 2):
                    w = first_channel[m]
                    wait(pe, "gelu_done", m + 1)
                    if not is_slot(n):
                        wait(pe, "y_done", m - 2)
                    for c in range(FC):
                        ins = pe.matmul(PY[m % 3], hid[:, m % 3, c * P:(c + 1) * P], w2[:, bass.ds(w + c * D, D)],
                                        start=(c == 0), stop=(c == FC - 1))
                    ins.then_inc(s["down_done"], 1)
                if is_slot(m := n + 1) and m % GROUP == 0:
                    _, found = nc.values_load_multi_w_load_instructions(
                        slot_w[0:1, m:m + GROUP], engines=[mybir.EngineType.PE], min_val=0, max_val=(E - 1) * F,
                        skip_runtime_bounds_check_because="VectorE clamps the expert to 0 .. E - 1")
                    first_channel[m:m + GROUP] = found


_INS = ["L0_attn_x_t", "L0_attn_W", "L0_ffn_gate_w", "L0_ffn_w1", "L0_ffn_w2"]


def kernel(**inputs):
    import numpy as _np
    import concourse.bacc as _bacc
    from concourse import mybir as _mybir
    from concourse.bass_utils import run_bass_kernel_spmd as _run

    nc = _bacc.Bacc("TRN2", target_bir_lowering=False, num_devices=1)
    arrays, args = {}, []
    for name in _INS:
        a = _np.ascontiguousarray(inputs[name])
        arrays[f"in_{name}_dram"] = a
        args.append(nc.dram_tensor(f"in_{name}_dram", a.shape, _mybir.dt.from_np(a.dtype), kind="ExternalInput").ap())
    args.append(nc.dram_tensor("out_0_dram", inputs["L0_attn_x_t"].shape, _mybir.dt.float32, kind="ExternalOutput").ap())
    build_gru_and_routed_ffn(nc, *args)
    r = _run(nc, [arrays], core_ids=[0])
    return r.results[0]["out_0_dram"]
```
